# Optimizing a Trainium2 kernel written in Bass

```python
import numpy as np
import jax
import jax.numpy as jnp

def _softmax(x, axis=-1):
    return jax.nn.softmax(x, axis=axis)

def _gelu(x):
    return jax.nn.gelu(x, approximate=True)

def _silu(x):
    return jax.nn.silu(x)

def _sigmoid(x):
    return jax.nn.sigmoid(x)

def _layernorm(x, axis=-1, eps=1e-05):
    m = jnp.mean(x, axis=axis, keepdims=True)
    v = jnp.var(x, axis=axis, keepdims=True)
    return (x - m) / jnp.sqrt(v + eps)

def _scatter_add(tgt, idx, src, axis=0):
    return tgt.at[idx].add(src)

def _segment_sum(src, seg, n):
    return jax.ops.segment_sum(src, seg, n)
kernel_name = 'mk_gnn_resnorm_d4_gnn_r64_479ba3'

def setup_inputs(seed: int=0):
    np.random.seed(seed)
    _w = jnp.asarray

    def _rec_inputs():
        import jax
        import jax.numpy as jnp
        _gk = jax.random.key(seed)
        x = -0.000202 + 1 * jax.random.normal(jax.random.fold_in(_gk, 1), (100000, 64), jnp.float32)
        src = jax.random.randint(jax.random.fold_in(_gk, 2), (50000,), 0, 100000, jnp.int32)
        dst = jax.random.randint(jax.random.fold_in(_gk, 3), (50000,), 0, 100000, jnp.int32)
        _o = jnp.argsort(dst, stable=True)
        src = src[_o]
        dst = dst[_o]
        edge_attr_16 = 5.96457e-05 + 0.999887 * jax.random.normal(jax.random.fold_in(_gk, 12), (50000, 16), jnp.float32)
        return (x, src, dst, edge_attr_16)
    x, src, dst, edge_attr_16 = _rec_inputs()

    def _L0_gnn_setup():
        import jax, jax.numpy as jnp
        import numpy as np
        N = 100000
        E = 25000
        D_IN = 64
        D_HID = 64
        D_OUT = 64

        def _gcn_norm(edge_index, num_nodes):
            loops = jnp.arange(num_nodes, dtype=edge_index.dtype)
            row = jnp.concatenate([edge_index[0], loops])
            col = jnp.concatenate([edge_index[1], loops])
            ones = jnp.ones(row.shape[0], dtype=jnp.float32)
            deg = jax.ops.segment_sum(ones, col, num_segments=num_nodes)
            dis = jnp.where(deg > 0, jax.lax.rsqrt(deg), 0.0)
            norm = dis[row] * dis[col]
            return (row, col, norm)

        def _gcn_conv(h, W, b, row, col, norm, num_nodes):
            h = h @ W.T
            msg = h[row] * norm[:, None]
            out = jax.ops.segment_sum(msg, col, num_segments=num_nodes)
            return out + b
        key = jax.random.key(seed)
        k_x, k_src, k_dst, k_w1, k_b1, k_w2, k_b2 = jax.random.split(key, 7)
        x = jax.random.normal(k_x, (N, D_IN), dtype=jnp.float32)
        src = jax.random.randint(k_src, (E,), 0, N, dtype=jnp.int64)
        dst = jax.random.randint(k_dst, (E,), 0, N, dtype=jnp.int64)
        edge_index = jnp.stack([src, dst], axis=0)
        s1 = 1.0 / np.sqrt(D_IN)
        s2 = 1.0 / np.sqrt(D_HID)
        W1 = jax.random.uniform(k_w1, (D_HID, D_IN), jnp.float32, -s1, s1)
        b1 = jax.random.uniform(k_b1, (D_HID,), jnp.float32, -s1, s1)
        W2 = jax.random.uniform(k_w2, (D_OUT, D_HID), jnp.float32, -s2, s2)
        b2 = jax.random.uniform(k_b2, (D_OUT,), jnp.float32, -s2, s2)
        return {'x': x, 'edge_index': edge_index, 'W1': W1, 'b1': b1, 'W2': W2, 'b2': b2}
    _L0_gnn_all = _L0_gnn_setup()
    _L0_gnn_in = {k: v for k, v in _L0_gnn_all.items() if k in ('W1', 'b1', 'W2', 'b2')}
    del _L0_gnn_all

    def _L1_gnn_setup():
        import jax, jax.numpy as jnp
        import numpy as np
        N_NODES = 100000
        N_EDGES = 12500
        D_IN = 64
        D_OUT = 64
        NEG_SLOPE = 0.1
        key = jax.random.key(seed)
        k1, k2, k3 = jax.random.split(key, 3)
        x = jax.random.normal(k1, (N_NODES, D_IN), dtype=jnp.float32)
        edge_index = jax.random.randint(k2, (2, N_EDGES), 0, N_NODES, dtype=jnp.int64)
        scale = jnp.sqrt(6.0 / (D_IN + D_OUT)).astype(jnp.float32)
        weight = jax.random.uniform(k3, (D_IN, D_OUT), dtype=jnp.float32, minval=-scale, maxval=scale)
        bias = jnp.zeros((D_OUT,), dtype=jnp.float32)
        return {'x': x, 'edge_index': edge_index, 'weight': weight, 'bias': bias}
    _L1_gnn_all = _L1_gnn_setup()
    _L1_gnn_in = {k: v for k, v in _L1_gnn_all.items() if k in ('weight', 'bias')}
    del _L1_gnn_all

    def _L2_gnn_setup():
        import jax, jax.numpy as jnp
        import numpy as np
        N_NODES = 20000
        N_EDGES = 10000
        H = 64
        E_FEAT = 16
        T = 2

        def _gru_cell(a, h, W_ih, W_hh, b_ih, b_hh):
            gi = a @ W_ih.T + b_ih
            gh = h @ W_hh.T + b_hh
            i_r, i_z, i_n = jnp.split(gi, 3, axis=1)
            h_r, h_z, h_n = jnp.split(gh, 3, axis=1)
            r = jax.nn.sigmoid(i_r + h_r)
            z = jax.nn.sigmoid(i_z + h_z)
            n = jnp.tanh(i_n + r * h_n)
            return (1.0 - z) * n + z * h
        key = jax.random.key(seed)
        ks = jax.random.split(key, 10)
        hv = jax.random.normal(ks[0], (N_NODES, H), dtype=jnp.float32)
        e = jax.random.normal(ks[1], (N_EDGES, E_FEAT), dtype=jnp.float32)
        src = jax.random.randint(ks[2], (N_EDGES,), 0, N_NODES, dtype=jnp.int32)
        dst = jax.random.randint(ks[3], (N_EDGES,), 0, N_NODES, dtype=jnp.int32)
        s = 0.1
        W_msg = jax.random.normal(ks[4], (T, 2 * H + E_FEAT, 2 * H), dtype=jnp.float32) * s
        b_msg = jax.random.normal(ks[5], (T, 2 * H), dtype=jnp.float32) * s
        W_ih = jax.random.normal(ks[6], (T, 3 * H, 2 * H), dtype=jnp.float32) * s
        W_hh = jax.random.normal(ks[7], (T, 3 * H, H), dtype=jnp.float32) * s
        b_ih = jax.random.normal(ks[8], (T, 3 * H), dtype=jnp.float32) * s
        b_hh = jax.random.normal(ks[9], (T, 3 * H), dtype=jnp.float32) * s
        return {'hv': hv, 'e': e, 'src': src, 'dst': dst, 'W_msg': W_msg, 'b_msg': b_msg, 'W_ih': W_ih, 'W_hh': W_hh, 'b_ih': b_ih, 'b_hh': b_hh}
    _L2_gnn_all = _L2_gnn_setup()
    _L2_gnn_in = {k: v for k, v in _L2_gnn_all.items() if k in ('W_msg', 'b_msg', 'W_ih', 'W_hh', 'b_ih', 'b_hh')}
    del _L2_gnn_all

    def _L3_gnn_setup():
        import jax, jax.numpy as jnp
        import numpy as np
        N_NODES = 100000
        N_EDGES = 25000
        D = 64
        key = jax.random.key(seed)
        k1, k2, k3 = jax.random.split(key, 3)
        z = jax.random.normal(k1, (N_NODES, D), dtype=jnp.float32)
        ei = jax.random.randint(k2, (2, N_EDGES), 0, N_NODES, dtype=jnp.int32)
        W = jax.random.normal(k3, (D, D), dtype=jnp.float32) * (1.0 / np.sqrt(D))
        b = jnp.zeros((D,), dtype=jnp.float32)
        return {'z': z, 'ei': ei, 'W': W, 'b': b}
    _L3_gnn_all = _L3_gnn_setup()
    _L3_gnn_in = {k: v for k, v in _L3_gnn_all.items() if k in ('W', 'b')}
    del _L3_gnn_all
    return {'x': x, 'src': src, 'dst': dst, 'edge_attr_16': edge_attr_16, 'L0_gnn_W1': _L0_gnn_in['W1'], 'L0_gnn_b1': _L0_gnn_in['b1'], 'L0_gnn_W2': _L0_gnn_in['W2'], 'L0_gnn_b2': _L0_gnn_in['b2'], 'L1_gnn_weight': _L1_gnn_in['weight'], 'L1_gnn_bias': _L1_gnn_in['bias'], 'L2_gnn_W_msg': _L2_gnn_in['W_msg'], 'L2_gnn_b_msg': _L2_gnn_in['b_msg'], 'L2_gnn_W_ih': _L2_gnn_in['W_ih'], 'L2_gnn_W_hh': _L2_gnn_in['W_hh'], 'L2_gnn_b_ih': _L2_gnn_in['b_ih'], 'L2_gnn_b_hh': _L2_gnn_in['b_hh'], 'L3_gnn_W': _L3_gnn_in['W'], 'L3_gnn_b': _L3_gnn_in['b']}

def reference(x, src, dst, edge_attr_16, L0_gnn_W1, L0_gnn_b1, L0_gnn_W2, L0_gnn_b2, L1_gnn_weight, L1_gnn_bias, L2_gnn_W_msg, L2_gnn_b_msg, L2_gnn_W_ih, L2_gnn_W_hh, L2_gnn_b_ih, L2_gnn_b_hh, L3_gnn_W, L3_gnn_b):
    import jax
    import jax.numpy as jnp

    def _L0_gnn_ref(x, edge_index, W1, b1, W2, b2):
        import jax, jax.numpy as jnp
        import numpy as np
        N = 100000
        E = 25000
        D_IN = 64
        D_HID = 64
        D_OUT = 64

        def _gcn_norm(edge_index, num_nodes):
            loops = jnp.arange(num_nodes, dtype=edge_index.dtype)
            row = jnp.concatenate([edge_index[0], loops])
            col = jnp.concatenate([edge_index[1], loops])
            ones = jnp.ones(row.shape[0], dtype=jnp.float32)
            deg = jax.ops.segment_sum(ones, col, num_segments=num_nodes)
            dis = jnp.where(deg > 0, jax.lax.rsqrt(deg), 0.0)
            norm = dis[row] * dis[col]
            return (row, col, norm)

        def _gcn_conv(h, W, b, row, col, norm, num_nodes):
            h = h @ W.T
            msg = h[row] * norm[:, None]
            out = jax.ops.segment_sum(msg, col, num_segments=num_nodes)
            return out + b
        num_nodes = x.shape[0]
        row, col, norm = _gcn_norm(edge_index, num_nodes)
        h = _gcn_conv(x, W1, b1, row, col, norm, num_nodes)
        h = jax.nn.relu(h)
        out = _gcn_conv(h, W2, b2, row, col, norm, num_nodes)
        return out

    def _L1_gnn_ref(x, edge_index, weight, bias):
        import jax, jax.numpy as jnp
        import numpy as np
        N_NODES = 100000
        N_EDGES = 12500
        D_IN = 64
        D_OUT = 64
        NEG_SLOPE = 0.1
        n = x.shape[0]
        loops = jnp.arange(n, dtype=edge_index.dtype)
        src = jnp.concatenate([edge_index[0], loops])
        dst = jnp.concatenate([edge_index[1], loops])
        h = x @ weight
        deg = jax.ops.segment_sum(jnp.ones_like(dst, dtype=h.dtype), dst, num_segments=n)
        deg_inv_sqrt = jnp.where(deg > 0, jax.lax.rsqrt(deg), 0.0)
        norm = deg_inv_sqrt[src] * deg_inv_sqrt[dst]
        msgs = h[src] * norm[:, None]
        out = jax.ops.segment_sum(msgs, dst, num_segments=n)
        out = out + bias
        return jnp.where(out >= 0, out, NEG_SLOPE * out)

    def _L2_gnn_ref(hv, e, src, dst, W_msg, b_msg, W_ih, W_hh, b_ih, b_hh):
        import jax, jax.numpy as jnp
        import numpy as np
        N_NODES = 20000
        N_EDGES = 10000
        H = 64
        E_FEAT = 16
        T = 2

        def _gru_cell(a, h, W_ih, W_hh, b_ih, b_hh):
            gi = a @ W_ih.T + b_ih
            gh = h @ W_hh.T + b_hh
            i_r, i_z, i_n = jnp.split(gi, 3, axis=1)
            h_r, h_z, h_n = jnp.split(gh, 3, axis=1)
            r = jax.nn.sigmoid(i_r + h_r)
            z = jax.nn.sigmoid(i_z + h_z)
            n = jnp.tanh(i_n + r * h_n)
            return (1.0 - z) * n + z * h
        num_nodes = hv.shape[0]
        num_rounds = W_msg.shape[0]
        for t in range(num_rounds):
            msg_in = jnp.concatenate([hv[dst], hv[src], e], axis=1)
            msgs = msg_in @ W_msg[t] + b_msg[t]
            a = jax.ops.segment_sum(msgs, dst, num_segments=num_nodes)
            hv = _gru_cell(a, hv, W_ih[t], W_hh[t], b_ih[t], b_hh[t])
        return hv

    def _L3_gnn_ref(z, ei, W, b):
        import jax, jax.numpy as jnp
        import numpy as np
        N_NODES = 100000
        N_EDGES = 25000
        D = 64
        N = z.shape[0]
        loops = jnp.arange(N, dtype=ei.dtype)
        src = jnp.concatenate([ei[0], loops])
        dst = jnp.concatenate([ei[1], loops])
        deg = jax.ops.segment_sum(jnp.ones_like(dst, dtype=z.dtype), dst, num_segments=N)
        dinv = jnp.where(deg > 0, jax.lax.rsqrt(deg), 0.0)
        norm = dinv[src] * dinv[dst]
        x = z @ W.T
        msg = x[src] * norm[:, None]
        out = jax.ops.segment_sum(msg, dst, num_segments=N) + b
        return jax.nn.relu(out)
    edge_index = jnp.stack([src, dst])
    x = _layernorm(x + _L0_gnn_ref(x, edge_index, L0_gnn_W1, L0_gnn_b1, L0_gnn_W2, L0_gnn_b2), axis=-1)
    x = _layernorm(x + _L1_gnn_ref(x, edge_index, L1_gnn_weight, L1_gnn_bias), axis=-1)
    x = _layernorm(x + _L2_gnn_ref(x, edge_attr_16, src, dst, L2_gnn_W_msg, L2_gnn_b_msg, L2_gnn_W_ih, L2_gnn_W_hh, L2_gnn_b_ih, L2_gnn_b_hh), axis=-1)
    x = _layernorm(x + _L3_gnn_ref(x, edge_index, L3_gnn_W, L3_gnn_b), axis=-1)
    return x

_drawn_inputs = setup_inputs


def setup_inputs(seed=0):
    import zlib

    import numpy as np

    out = dict(_drawn_inputs(seed))
    spreads = {'L1_gnn_bias': (0.0, 0.1), 'L3_gnn_b': (0.0, 0.1)}
    factors = {}
    for name, (base, spread) in spreads.items():
        noise = np.random.default_rng([zlib.crc32(name.encode()), seed]).standard_normal(out[name].shape)
        drawn = base * np.exp(spread * noise) if base else spread * noise
        out[name] = jnp.asarray(drawn.astype(out[name].dtype))
    for name, factor in factors.items():
        out[name] = (out[name] * factor).astype(out[name].dtype)
    return out
```

```python
import concourse.bass as bass
from concourse import mybir
from contextlib import ExitStack

N = 100000
E = 50000
D = 64
DE = 16
P = 128
NPP = 8
TILE = P * NPP
TILES = -(-N // TILE)
NPAD = TILES * TILE
LASTP = (N - (TILES - 1) * TILE) // NPP
GC = 7
HALF = -(-E // (P * GC * 2))
GROUPS = 2 * HALF
CHUNKS = GROUPS * GC
CB = -(-CHUNKS // P)
LASTC = CHUNKS - (CB - 1) * P
AW = DE + 1
KB = D + AW + 2
GW = 4 * D
FAR = float(1 << 20)
EPS = 1e-5
LAYERS = 6
GRU = (3, 4)
LN = (1, 2, 4, 5)
LOADS = (3, 4, 3, 3, 4, 3)
UNITS = 2 * TILES
HN = NPP // 2


def build(nc, t):
    f32, i32 = mybir.dt.float32, mybir.dt.int32
    ALU, ACT, AX = mybir.AluOpType, mybir.ActivationFunctionType, mybir.AxisListType
    with ExitStack() as ctx:
        def sb(name, shape, dt=f32):
            return ctx.enter_context(nc.sbuf_tensor(name, shape, dt))

        def two(name, shape, dt=f32):
            return [sb(f"{name}{q}", shape, dt) for q in range(2)]

        def sem(name):
            return ctx.enter_context(nc.semaphore(name))

        def sems(name):
            return [sem(f"{name}{q}") for q in range(2)]

        def dram(name, shape):
            return nc.dram_tensor(name, shape, f32).ap()

        agg = dram("agg", (NPAD, D))
        aux = dram("aux", (NPAD, AW))
        carry = dram("carry", (CHUNKS, D))
        carry_aux = dram("carry_aux", (CHUNKS, AW))
        s_tab = dram("s_tab", (NPAD, 1))
        h1, x1, x2, v1, x3 = (dram(n, (NPAD, D)) for n in ("h1", "x1", "x2", "v1", "x3"))
        layer_in = [t["x"], h1, x1, x2, v1, x3]
        layer_res = [None, t["x"], None, None, x2, None]
        layer_out = [h1, x1, x2, v1, x3, t["out"]]

        lane_i = sb("lane_i", [P, P], i32)
        lane = sb("lane", [P, P])
        part_i = sb("part_i", [P, 1], i32)
        part = sb("part", [P, 1])
        ident = sb("ident", [P, P])
        src_c = sb("src_c", [P, CHUNKS], i32)
        dst_r = sb("dst_r", [P, CB * P], i32)
        prv_r = sb("prv_r", [P, CB * P], i32)
        back_r = sb("back_r", [P, CB], i32)
        head_r = sb("head_r", [P, CB * P], i32)
        dstf = sb("dstf", [P, CB, P])
        prvf = sb("prvf", [P, CB, P])
        backf = sb("backf", [P, CB])
        headf = sb("headf", [P, CB * P])
        begin = sb("begin", [P, CB, P])
        first = two("first", [P, CB, P])
        sidx_r = sb("sidx_r", [P, CB, P])
        first_c = sb("first_c", [P, CB * P])
        dst_idx = sb("dst_idx", [P, CB * P], i32)
        cont = sb("cont", [P, CB])
        lead = sb("lead", [P, CB])
        cidx_f = sb("cidx_f", [P, CB])
        carry_src = sb("carry_src", [P, CB], i32)
        carry_dst = sb("carry_dst", [P, CB], i32)
        same = sb("same", [P, CB, CB * P])
        edge_w = sb("edge_w", [P, CHUNKS])
        deg = sb("deg", [P, NPAD // P])
        eps = sb("eps", [P, 1])
        s_big = sb("s_big", [P, NPAD // P])
        WB = NPAD // P // 8
        wide = sb("wide", [P, WB * D])
        BW = [sb(f"bw{l}", [P, P]) for l in range(4)]
        bias = [sb(f"bias{l}", [P, D]) for l in range(4)]
        wms = [sb(f"wms{r}", [P, D]) for r in range(2)]
        wmd = [sb(f"wmd{r}", [P, D + AW]) for r in range(2)]
        wih = [sb(f"wih{r}", [P, 3 * D]) for r in range(2)]
        RA = [sb(f"ra{r}", [P, GW]) for r in range(2)]
        RB = [sb(f"rb{r}", [KB, GW]) for r in range(2)]

        src_st = two("src_st", [P, GC], i32)
        dst_st = two("dst_st", [P, GC], i32)
        rows = two("rows", [P, GC, D])
        erows = two("erows", [P, GC, AW])
        w_st = two("w_st", [P, GC])
        sel = two("sel", [P, GC, P])
        sums = two("sums", [P, GC, D])
        esums = two("esums", [P, GC, AW])
        cbuf = sb("cbuf", [P, CB, D])
        cbuf_aux = sb("cbuf_aux", [P, CB, AW])
        cold = sb("cold", [P, CB, D])
        cold_aux = sb("cold_aux", [P, CB, AW])
        cnew = sb("cnew", [P, CB, D])
        cnew_aux = sb("cnew_aux", [P, CB, AW])

        h_t = two("h_t", [P, NPP, D])
        agg_t = two("agg_t", [P, NPP, D])
        res_t = two("res_t", [P, NPP, D])
        s_t = two("s_t", [P, NPP])
        aux_t = two("aux_t", [P, NPP, AW])
        y_t = two("y_t", [P, NPP, D])
        y1_t = two("y1_t", [P, NPP, D])
        yT = two("yT", [P, NPP * D])
        z_t = two("z_t", [P, NPP, D])
        xc_t = two("xc_t", [P, NPP, D])
        sq_t = two("sq_t", [P, NPP, D])
        o_t = two("o_t", [P, NPP, D])
        st_t = two("st_t", [P, 4, NPP])
        ah_t = two("ah_t", [P, NPP, 2 * D])
        b_t = two("b_t", [P, NPP, KB])
        aT = two("aT", [P, HN * P])
        bT = two("bT", [KB, HN * P])
        rz_t = two("rz_t", [P, HN, 2 * D])
        n_t = two("n_t", [P, HN, D])
        m_t = two("m_t", [P, HN, D])
        d_t = two("d_t", [P, HN, D])
        d2_t = two("d2_t", [P, HN, D])
        d3_t = two("d3_t", [P, HN, D])

        psA = [ctx.enter_context(nc.psum_tensor(f"psA{q}", [P, 512], f32)) for q in range(2)]
        psB = [ctx.enter_context(nc.psum_tensor(f"psB{q}", [P, 512], f32)) for q in range(2)]
        psG = [ctx.enter_context(nc.psum_tensor(f"psG{q}", [P, HN, GW], f32)) for q in range(2)]

        in_loaded = sem("in_loaded")
        bw_zeroed = sem("bw_zeroed")
        bw_loaded = sem("bw_loaded")
        zeros_set = sem("zeros_set")
        tabs_zeroed = sem("tabs_zeroed")
        iotas = sem("iotas")
        prep = sem("prep")
        prep_t = sem("prep_t")
        prep_w = sem("prep_w")
        fold_mm = sem("fold_mm")
        ones_set = sem("ones_set")
        bias_rows = sem("bias_rows")
        aux_loaded = sem("aux_loaded")
        s_done = sem("s_done")
        deg_root = sem("deg_root")
        s_ready = sem("s_ready")
        eps_set = sem("eps_set")
        s_stored = sem("s_stored")
        src_staged, dst_staged = sems("src_staged"), sems("dst_staged")
        gathered, e_loaded = sems("gathered"), sems("e_loaded")
        w_copied, sel_built = sems("w_copied"), sems("sel_built")
        combined, sums_out = sems("combined"), sems("sums_out")
        scattered, carried = sems("scattered"), sems("carried")
        pool_turn = sem("pool_turn")
        c_loaded, c_combined, c_gathered = sem("c_loaded"), sem("c_combined"), sem("c_gathered")
        c_added, c_scattered = sem("c_added"), sem("c_scattered")
        loaded, stored = sems("loaded"), sems("stored")
        finished = sem("finished")
        y_scaled, y_summed, y_ready = sem("y_scaled"), sem("y_summed"), sem("y_ready")
        y_transposed, yT_ready, mm_done = sem("y_transposed"), sem("yT_ready"), sem("mm_done")
        z_biased, z_acted, z_ready = sem("z_biased"), sem("z_acted"), sem("z_ready")
        n_sum, n_mean, n_centred = sem("n_sum"), sem("n_mean"), sem("n_centred")
        n_squared, n_var, n_std, n_rstd = sem("n_squared"), sem("n_var"), sem("n_std"), sem("n_rstd")
        b_ready, g_transposed = sem("b_ready"), sem("g_transposed")
        aT_ready, bT_ready, g_mm = sem("aT_ready"), sem("bT_ready"), sem("g_mm")
        gates, n_prod, n_pre, n_act = sem("gates"), sem("n_prod"), sem("n_pre"), sem("n_act")
        g_diff, g_scaled, g_new = sem("g_diff"), sem("g_scaled"), sem("g_new")

        def edge_base(p):
            return 0 if p == "aux" else HALF * (1 + p)

        def gather_base(p):
            return 0 if p == "w" else HALF * (1 + p)

        def carry_no(p):
            return 0 if p == "aux" else 1 + p

        def gcn_base(l):
            return TILES * sum(k not in GRU for k in range(l))

        def ln_base(l):
            return TILES * sum(k in LN for k in range(l))

        def gru_base(l):
            return UNITS * sum(k in GRU for k in range(l))

        def load_base(l):
            return 16 * (TILES // 2) * sum(LOADS[:l])

        def walk(eng, n, body):
            body(0)
            with eng.Fori(1, n - 1) as i:
                body(i)
            body(n - 1)

        def peeled(i):
            return isinstance(i, int)

        BT = TILES // 2
        in_names = ("src_cols", "dst_rows", "prev_rows", "back", "head")
        PREP_LOADS = len(in_names) + 4 + 2 * 3
        C_ROWS = CB

        block = ctx.enter_context(nc.Block())

        @block.sync
        def _(sp):
            for name, buf in zip(in_names, (src_c, dst_r, prv_r, back_r, head_r)):
                sp.dma_start(buf[:, :], t[name]).then_inc(in_loaded, 16)
            for l in range(4):
                sp.dma_start(bias[l][:, :], t[f"bias{l}"]).then_inc(in_loaded, 16)
            for r in range(2):
                sp.dma_start(wms[r][:, :], t[f"wms{r}"]).then_inc(in_loaded, 16)
                sp.dma_start(wmd[r][:, :], t[f"wmd{r}"]).then_inc(in_loaded, 16)
                sp.dma_start(wih[r][:, :], t[f"wih{r}"]).then_inc(in_loaded, 16)
            sp.wait_ge(bw_zeroed, 1)
            for l in range(4):
                sp.dma_start(BW[l][0:D, 0:D], t[f"w{l}"]).then_inc(bw_loaded, 16)
                sp.dma_start(BW[l][D:P, D:P], t[f"w{l}"]).then_inc(bw_loaded, 16)
            for r in range(2):
                sp.dma_start(RA[r][D:P, 0:2 * D], t[f"whh{r}"][:, 0:2 * D]).then_inc(bw_loaded, 16)
                sp.dma_start(RA[r][D:P, 3 * D:GW], t[f"whh{r}"][:, 2 * D:3 * D]).then_inc(bw_loaded, 16)
            sp.wait_ge(zeros_set, 1)
            for k in range(8):
                sp.dma_start(agg.rearrange("(p k) d -> p (k d)", p=P)[:, k * WB * D:(k + 1) * WB * D],
                             wide[:, :]).then_inc(tabs_zeroed, 16)
            for k in range(8):
                sp.dma_start(aux.rearrange("(p k) d -> p (k d)", p=P)[:, k * WB * AW:(k + 1) * WB * AW],
                             wide[:, 0:WB * AW]).then_inc(tabs_zeroed, 16)
            sp.wait_ge(ones_set, 1)
            for r in range(2):
                sp.dma_start(RB[r][KB - 2:KB, :], t[f"gbias{r}"]).then_inc(bias_rows, 16)

            def edge_pass(p):
                out, table, w = (esums, carry_aux, AW) if p == "aux" else (sums, carry, D)

                def body(i):
                    for q in range(2):
                        n = edge_base(p) + i
                        if p == "aux":
                            if not (peeled(i) and i == 0):
                                sp.wait_ge(combined[q], n)
                            e0 = (i * 2 + q) * (GC * P)
                            sp.dma_start(erows[q][:, :, 0:DE], t["edges"][bass.ds(e0, GC * P), :]
                                         .rearrange("(c p) d -> p c d", p=P)).then_inc(e_loaded[q], 16)
                    for q in range(2):
                        n = edge_base(p) + i
                        sp.wait_ge(sums_out[q], n + 1)
                        sp.dma_start(table[bass.ds((i * 2 + q) * GC, GC), :].rearrange("(a c) d -> a c d", a=1),
                                     out[q][0:1, :, :]).then_inc(carried[q], 16)
                walk(sp, HALF, body)
                for q in range(2):
                    sp.wait_ge(carried[q], 16 * (edge_base(p) + HALF))
                dst = cbuf_aux if p == "aux" else cbuf
                full = (CB - 1) * P
                sp.dma_start(dst[:, 0:CB - 1, :], table[0:full, :].rearrange("(b p) d -> p b d", p=P)
                             ).then_inc(c_loaded, 16)
                sp.dma_start(dst[0:LASTC, CB - 1, :], table[full:CHUNKS, :]).then_inc(c_loaded, 16)

            edge_pass("aux")
            sp.wait_ge(c_scattered, 16 * C_ROWS)
            av = aux.rearrange("(p k) d -> p (k d)", p=P)
            for k in range(8):
                if k:
                    sp.wait_ge(s_done, k)
                sp.dma_start(wide[:, 0:WB * AW], av[:, k * WB * AW:(k + 1) * WB * AW]).then_inc(aux_loaded, 16)
            sp.wait_ge(s_ready, 1)
            sp.dma_start(s_tab.rearrange("(p k) a -> p (k a)", p=P), s_big[:, :]).then_inc(s_stored, 16)

            for l in range(LAYERS):
                edge_pass(l)
                sp.wait_ge(c_scattered, 16 * C_ROWS * (carry_no(l) + 1))

                def view(tab, tile, parts=P):
                    r = tile * TILE
                    return tab[bass.ds(r, parts * NPP), :].rearrange("(p j) d -> p j d", p=parts)

                def load(tile, q):
                    parts = LASTP if peeled(tile) and tile == TILES - 1 else P
                    if l in GRU:
                        sp.dma_start(ah_t[q][:, :, 0:D], view(agg, tile)).then_inc(loaded[q], 16)
                        sp.dma_start(ah_t[q][:, :, D:2 * D], view(layer_in[l], tile)).then_inc(loaded[q], 16)
                        sp.dma_start(aux_t[q][:, :, :], view(aux, tile)).then_inc(loaded[q], 16)
                    else:
                        ip = parts if l == 0 else P
                        sp.dma_start(agg_t[q][:, :, :], view(agg, tile)).then_inc(loaded[q], 16)
                        sp.dma_start(h_t[q][0:ip, :, :], view(layer_in[l], tile, ip)).then_inc(loaded[q], 16)
                        sp.dma_start(s_t[q][:, :], s_tab[bass.ds(tile * TILE, TILE), :]
                                     .rearrange("(p j) a -> p (j a)", p=P)).then_inc(loaded[q], 16)
                    if layer_res[l] is not None:
                        ip = parts if l == 1 else P
                        sp.dma_start(res_t[q][0:ip, :, :], view(layer_res[l], tile, ip)).then_inc(loaded[q], 16)

                def store(tile, q):
                    last = peeled(tile) and tile == TILES - 1
                    ip = LASTP if last and l == LAYERS - 1 else P
                    sp.dma_start(view(layer_out[l], tile, ip), o_t[q][0:ip, :, :]).then_inc(stored[q], 16)

                for q in range(2):
                    load(q, q)

                def body(i):
                    for q in range(2):
                        sp.wait_ge(finished, TILES * l + i * 2 + q + 1)
                        store(i * 2 + q, q)
                        if not (peeled(i) and i == BT - 1):
                            load(i * 2 + q + 2, q)
                body(0)
                with sp.Fori(1, BT - 2) as i:
                    body(i)
                body(BT - 2)
                body(BT - 1)
                for q in range(2):
                    sp.wait_ge(stored[q], 16 * BT * (l + 1))

        @block.gpsimd
        def _(pool):
            nc.gpsimd.iota(lane_i[:, :], pattern=[[1, P]], base=0, channel_multiplier=0).then_inc(iotas, 1)
            nc.gpsimd.iota(part_i[:, :], pattern=[[0, 1]], base=0, channel_multiplier=1).then_inc(iotas, 1)
            for q in range(2):
                nc.gpsimd.memset(b_t[q][:, :, :], 1.0).then_inc(iotas, 1)
            for b in (h_t[1], res_t[1]):
                nc.gpsimd.memset(b[:, :, :], 0.0).then_inc(iotas, 1)
            pool.wait_ge(prep, 1)

            def gather_group(p, q, n):
                pool.wait_ge(src_staged[q], n + 1)
                pool.sem_inc(pool_turn, 1)
                tab = s_tab if p == "w" else layer_in[p]
                for c in range(GC):
                    dst = w_st[q][:, c:c + 1] if p == "w" else rows[q][:, c, :]
                    nc.gpsimd.indirect_dma_start(dst, None, tab, bass.IndirectOffsetOnAxis(
                        ap=src_st[q][:, c:c + 1], axis=0)).then_inc(gathered[q], 16)

            def scatter_group(p, q, i):
                out, tab = (esums, aux) if p == "aux" else (sums, agg)
                n = edge_base(p) + i
                pool.wait_ge(dst_staged[q], n + 1)
                pool.wait_ge(sums_out[q], n + 1)
                pool.sem_inc(pool_turn, 1)
                for c in range(GC):
                    nc.gpsimd.indirect_dma_start(tab, bass.IndirectOffsetOnAxis(
                        ap=dst_st[q][:, c:c + 1], axis=0), out[q][:, c, :], None,
                        bounds_check=N - 1, oob_is_err=False).then_inc(scattered[q], 16)

            def carry_stage(p):
                old, new, tab = (cold_aux, cnew_aux, aux) if p == "aux" else (cold, cnew, agg)
                for q in range(2):
                    pool.wait_ge(scattered[q], 16 * GC * (edge_base(p) + HALF))
                for b in range(CB):
                    nc.gpsimd.indirect_dma_start(old[:, b, :], None, tab, bass.IndirectOffsetOnAxis(
                        ap=carry_src[:, b:b + 1], axis=0), bounds_check=N - 1, oob_is_err=False
                        ).then_inc(c_gathered, 16)
                pool.wait_ge(c_added, carry_no(p) + 1)
                for b in range(CB):
                    nc.gpsimd.indirect_dma_start(tab, bass.IndirectOffsetOnAxis(
                        ap=carry_dst[:, b:b + 1], axis=0), new[:, b, :], None,
                        bounds_check=N - 1, oob_is_err=False).then_inc(c_scattered, 16)

            pool.wait_ge(tabs_zeroed, 16 * 16)
            walk(pool, HALF, lambda i: [scatter_group("aux", q, i) for q in range(2)])
            carry_stage("aux")

            pool.wait_ge(s_stored, 16)
            walk(pool, HALF, lambda i: [gather_group("w", q, gather_base("w") + i) for q in range(2)])

            for l in range(LAYERS):
                if l:
                    for q in range(2):
                        pool.wait_ge(stored[q], 16 * BT * l)
                for q in range(2):
                    gather_group(l, q, gather_base(l))

                def body(i):
                    for q in range(2):
                        scatter_group(l, q, i)
                        if not (peeled(i) and i == HALF - 1):
                            gather_group(l, q, gather_base(l) + i + 1)
                walk(pool, HALF, body)
                carry_stage(l)

                if l in GRU:
                    def body(i):
                        for q in range(2):
                            tile = i * 2 + q
                            pool.wait_ge(loaded[q], load_base(l) + (i + 1) * (16 * LOADS[l]))
                            nc.gpsimd.tensor_tensor(b_t[q][:, :, 0:D], ah_t[q][:, :, D:2 * D],
                                                    aux_t[q][:, :, DE:AW].to_broadcast([P, NPP, D]),
                                                    ALU.mult).then_inc(b_ready, 1)
                            nc.gpsimd.tensor_copy(b_t[q][:, :, D:D + AW], aux_t[q][:, :, :]).then_inc(b_ready, 1)
                            if l not in LN and not (peeled(i) and i == 0):
                                pool.wait_ge(stored[q], 16 * BT * l + i * 16)
                            for g in range(2):
                                n = gru_base(l) + i * 4 + q * 2 + g
                                out = z_t if l in LN else o_t
                                hv = ah_t[q][:, g * HN:(g + 1) * HN, D:2 * D]
                                pool.wait_ge(n_act, n + 1)
                                nc.gpsimd.tensor_tensor(d_t[g][:, :, :], hv, n_t[g][:, :, :],
                                                        ALU.subtract).then_inc(g_diff, 1)
                                pool.wait_ge(g_diff, n + 1)
                                nc.gpsimd.tensor_tensor(m_t[g][:, :, :], d_t[g][:, :, :], rz_t[g][:, :, D:2 * D],
                                                        ALU.mult).then_inc(g_scaled, 1)
                                pool.wait_ge(g_scaled, n + 1)
                                ins = nc.gpsimd.tensor_tensor(out[q][:, g * HN:(g + 1) * HN, :], m_t[g][:, :, :],
                                                              n_t[g][:, :, :], ALU.add)
                                if l in LN:
                                    ins.then_inc(g_new, 1)
                                elif g == 0:
                                    ins.then_inc(g_new, 1)
                                else:
                                    ins.then_inc(finished, 1)
                    walk(pool, BT, body)
                else:
                    def body(i):
                        for q in range(2):
                            n = gcn_base(l) + i * 2 + q
                            pool.wait_ge(loaded[q], load_base(l) + (i + 1) * (16 * LOADS[l]))
                            s_b = s_t[q][:, :].rearrange("p (j a) -> p j a", a=1).to_broadcast([P, NPP, D])
                            nc.gpsimd.tensor_tensor(y_t[q][:, :, :], h_t[q][:, :, :], s_b, ALU.mult
                                                    ).then_inc(y_scaled, 1)
                            pool.wait_ge(y_scaled, n + 1)
                            nc.gpsimd.tensor_tensor(y1_t[q][:, :, :], y_t[q][:, :, :], agg_t[q][:, :, :], ALU.add
                                                    ).then_inc(y_summed, 1)
                            pool.wait_ge(y_summed, n + 1)
                            nc.gpsimd.tensor_tensor(y_t[q][:, :, :], y1_t[q][:, :, :], s_b, ALU.mult
                                                    ).then_inc(y_ready, 1)
                    walk(pool, BT, body)

        @block.scalar
        def _(act):
            def edge_pass(p):
                out, w = (esums, AW) if p == "aux" else (sums, D)

                def body(i):
                    for q in range(2):
                        n = edge_base(p) + i
                        if not (p == "aux" and peeled(i) and i == 0):
                            act.wait_ge(scattered[q], n * (16 * GC))
                            act.wait_ge(carried[q], n * 16)
                        act.wait_ge(combined[q], n + 1)
                        nc.scalar.copy(out[q][:, :, :], psG[q][:, :, :].rearrange("p a b -> p (a b)")[:, 0:GC * w]
                                       .rearrange("p (c d) -> p c d", d=w)).then_inc(sums_out[q], 1)
                walk(act, HALF, body)

            edge_pass("aux")
            act.wait_ge(eps_set, 1)
            act.wait_ge(s_done, 8)
            nc.scalar.activation(deg[:, :], deg[:, :], ACT.Sqrt).then_inc(deg_root, 1)
            for l in range(LAYERS):
                edge_pass(l)
                if l in GRU:
                    def body(i):
                        for q in range(2):
                            for g in range(2):
                                n = gru_base(l) + i * 4 + q * 2 + g
                                act.wait_ge(g_transposed, n + 1)
                                nc.scalar.copy(aT[g][:, :], psA[g][:, :]).then_inc(aT_ready, 1)
                                act.wait_ge(g_mm, n + 1)
                                nc.scalar.activation(rz_t[g][:, :, :], psG[g][:, :, 0:2 * D], ACT.Sigmoid
                                                     ).then_inc(gates, 1)
                                act.wait_ge(n_pre, n + 1)
                                nc.scalar.activation(n_t[g][:, :, :], d2_t[g][:, :, :], ACT.Tanh).then_inc(n_act, 1)
                            if l in LN:
                                m = ln_base(l) + i * 2 + q
                                act.wait_ge(n_centred, m + 1)
                                nc.scalar.activation(sq_t[q][:, :, :], xc_t[q][:, :, :], ACT.Square
                                                     ).then_inc(n_squared, 1)
                                act.wait_ge(n_var, m + 1)
                                nc.scalar.activation(st_t[q][:, 3, :], st_t[q][:, 2, :], ACT.Sqrt,
                                                     bias=eps[:, 0:1], scale=1.0 / D).then_inc(n_std, 1)
                    walk(act, BT, body)
                else:
                    def body(i):
                        for q in range(2):
                            n = gcn_base(l) + i * 2 + q
                            act.wait_ge(y_transposed, n + 1)
                            nc.scalar.copy(yT[q][:, :], psA[q][:, :]).then_inc(yT_ready, 1)
                            if l == 0:
                                if not (peeled(i) and i == 0):
                                    act.wait_ge(stored[q], i * 16)
                                act.wait_ge(z_biased, n + 1)
                                nc.scalar.activation(o_t[q][:, :, :], z_t[q][:, :, :], ACT.Relu
                                                     ).then_inc(finished, 1)
                            else:
                                m = ln_base(l) + i * 2 + q
                                act.wait_ge(n_centred, m + 1)
                                nc.scalar.activation(sq_t[q][:, :, :], xc_t[q][:, :, :], ACT.Square
                                                     ).then_inc(n_squared, 1)
                                act.wait_ge(n_var, m + 1)
                                nc.scalar.activation(st_t[q][:, 3, :], st_t[q][:, 2, :], ACT.Sqrt,
                                                     bias=eps[:, 0:1], scale=1.0 / D).then_inc(n_std, 1)
                    walk(act, BT, body)

        @block.vector
        def _(dve):
            V = nc.vector
            for l in range(4):
                ins = V.memset(BW[l][:, :], 0.0)
            for r in range(2):
                ins = V.memset(RA[r][:, :], 0.0)
            ins.then_inc(bw_zeroed, 1)
            V.memset(wide[:, :], 0.0).then_inc(zeros_set, 1)
            V.memset(eps[:, :], EPS).then_inc(eps_set, 1)
            V.memset(cbuf[:, :, :], 0.0)
            V.memset(cbuf_aux[:, :, :], 0.0)
            V.memset(cold[:, :, :], 0.0)
            V.memset(cold_aux[:, :, :], 0.0)
            for r in range(2):
                V.memset(RB[r][:, :], 0.0)
            for q in range(2):
                V.memset(erows[q][:, :, :], 1.0)
            steps = [0]

            def link(ins):
                steps[0] += 1
                ins.then_inc(prep_w, 1)
                dve.wait_ge(prep_w, steps[0])

            dve.wait_ge(iotas, 6)
            V.tensor_copy(lane[:, :], lane_i[:, :])
            link(V.tensor_copy(part[:, :], part_i[:, :]))
            V.tensor_scalar(ident[:, :], lane[:, :], part[:, 0:1], None, ALU.is_equal)
            dve.wait_ge(in_loaded, 16 * PREP_LOADS)
            flat = "p a b -> p (a b)"
            V.tensor_copy(dstf[:, :, :].rearrange(flat), dst_r[:, :])
            V.tensor_copy(prvf[:, :, :].rearrange(flat), prv_r[:, :])
            V.tensor_copy(backf[:, :], back_r[:, :])
            link(V.tensor_copy(headf[:, :], head_r[:, :]))
            link(V.tensor_tensor(begin[:, :, :], dstf[:, :, :], prvf[:, :, :], ALU.not_equal))
            lanes = lane[:, :].rearrange("p (a l) -> p a l", a=1).to_broadcast([P, CB, P])
            link(V.tensor_tensor(first[0][:, :, :], begin[:, :, :], lanes, ALU.mult))
            k, a = 1, 0
            while k < P:
                V.tensor_copy(first[1 - a][:, :, 0:k], first[a][:, :, 0:k])
                link(V.tensor_tensor(first[1 - a][:, :, k:P], first[a][:, :, k:P], first[a][:, :, 0:P - k], ALU.max))
                k, a = 2 * k, 1 - a
            link(V.tensor_scalar(sidx_r[:, :, :], begin[:, :, :], -FAR, FAR, ALU.mult, ALU.add))
            link(V.tensor_tensor(first[1 - a][:, :, :], sidx_r[:, :, :], dstf[:, :, :], ALU.add))
            link(V.tensor_scalar(cont[:, :], begin[:, :, 0], -1.0, 1.0, ALU.mult, ALU.add))
            link(V.tensor_tensor(lead[:, :], backf[:, :], dstf[:, :, 0], ALU.not_equal))
            link(V.tensor_tensor(cidx_f[:, :], lead[:, :], cont[:, :], ALU.mult))
            link(V.tensor_scalar(lead[:, :], cidx_f[:, :], -FAR, FAR, ALU.mult, ALU.add))
            link(V.tensor_tensor(cidx_f[:, :], lead[:, :], dstf[:, :, 0], ALU.add))
            V.tensor_copy(carry_dst[:, :], cidx_f[:, :])
            V.tensor_copy(carry_src[:, :], dstf[:, :, 0])
            for b in range(CB):
                ins = V.tensor_scalar(same[:, b, :], headf[:, :], dstf[:, b, 0:1], cont[:, b:b + 1], ALU.is_equal,
                                      ALU.mult)
            ins.then_inc(prep_t, 1)
            dve.wait_ge(fold_mm, 1)
            V.tensor_copy(first_c[:, :], psA[0][:, :])
            V.tensor_copy(dst_idx[:, :], psA[1][:, :]).then_inc(prep, 1)
            dve.wait_ge(prep, 1)
            dve.wait_ge(fold_mm, 2)
            for r in range(2):
                V.tensor_copy(RA[r][0:D, 0:3 * D], psB[0][0:D, r * 3 * D:(r + 1) * 3 * D])
                ins = V.tensor_copy(RB[r][0:D + AW, 0:3 * D], psB[1][0:D + AW, r * 3 * D:(r + 1) * 3 * D])
            ins.then_inc(ones_set, 1)

            def stage_src(q, i, n):
                if not (peeled(i) and i == 0 and n == 0):
                    dve.wait_ge(gathered[q], n * (16 * GC))
                V.tensor_copy(src_st[q][:, :], src_c[:, bass.ds((i * 2 + q) * GC, GC)]).then_inc(src_staged[q], 1)

            def edge_pass(p):
                def body(i):
                    for q in range(2):
                        n = edge_base(p) + i
                        c0 = (i * 2 + q) * GC
                        if p != "aux":
                            stage_src(q, i, gather_base(p) + i)
                        begin_all = p == "aux" and peeled(i) and i == 0
                        if not begin_all:
                            dve.wait_ge(combined[q], n)
                        for c in range(GC):
                            if p == "aux" or p in GRU:
                                ins = V.tensor_scalar(sel[q][:, c, :], lane[:, :], first_c[:, bass.ds(c0 + c, 1)],
                                                      None, ALU.is_equal)
                            else:
                                ins = V.tensor_scalar(sel[q][:, c, :], lane[:, :], first_c[:, bass.ds(c0 + c, 1)],
                                                      edge_w[:, bass.ds(c0 + c, 1)], ALU.is_equal, ALU.mult)
                        ins.then_inc(sel_built[q], 1)
                        if not begin_all:
                            dve.wait_ge(scattered[q], n * (16 * GC))
                        V.tensor_copy(dst_st[q][:, :], dst_idx[:, bass.ds(c0, GC)]).then_inc(dst_staged[q], 1)
                walk(dve, HALF, body)
                old, new, w = (cold_aux, cnew_aux, AW) if p == "aux" else (cold, cnew, D)
                dve.wait_ge(c_combined, carry_no(p) + 1)
                dve.wait_ge(c_gathered, 16 * C_ROWS * (carry_no(p) + 1))
                V.tensor_tensor(new[:, :, :], old[:, :, :], psB[0][:, 0:CB * w].rearrange("p (b d) -> p b d", d=w),
                                ALU.add).then_inc(c_added, 1)

            edge_pass("aux")
            for k in range(8):
                dve.wait_ge(aux_loaded, 16 * (k + 1))
                V.tensor_scalar(deg[:, k * WB:(k + 1) * WB],
                                wide[:, 0:WB * AW].rearrange("p (k d) -> p k d", d=AW)[:, :, DE],
                                1.0, None, ALU.add).then_inc(s_done, 1)
            dve.wait_ge(deg_root, 1)
            V.reciprocal(s_big[:, :], deg[:, :]).then_inc(s_ready, 1)

            def w_copy(q, i):
                n = gather_base("w") + i
                dve.wait_ge(gathered[q], (n + 1) * (16 * GC))
                V.tensor_copy(edge_w[:, bass.ds((i * 2 + q) * GC, GC)], w_st[q][:, :]).then_inc(w_copied[q], 1)

            def w_body(i):
                for q in range(2):
                    if not (peeled(i) and i == 0):
                        w_copy(q, i - 1)
                    stage_src(q, i, gather_base("w") + i)
            walk(dve, HALF, w_body)
            for q in range(2):
                w_copy(q, HALF - 1)
                dve.wait_ge(w_copied[q], HALF)

            def layernorm(l, i, q):
                n = ln_base(l) + i * 2 + q
                z, xc, sq, st = z_t[q], xc_t[q], sq_t[q], st_t[q]
                bc = "p (j a) -> p j a"
                V.tensor_reduce(st[:, 0, :], z[:, :, :], AX.X, ALU.add).then_inc(n_sum, 1)
                dve.wait_ge(n_sum, n + 1)
                V.tensor_scalar(st[:, 1, :], st[:, 0, :], 1.0 / D, None, ALU.mult).then_inc(n_mean, 1)
                dve.wait_ge(n_mean, n + 1)
                V.tensor_tensor(xc[:, :, :], z[:, :, :], st[:, 1, :].rearrange(bc, a=1).to_broadcast([P, NPP, D]),
                                ALU.subtract).then_inc(n_centred, 1)
                dve.wait_ge(n_squared, n + 1)
                V.tensor_reduce(st[:, 2, :], sq[:, :, :], AX.X, ALU.add).then_inc(n_var, 1)
                dve.wait_ge(n_std, n + 1)
                V.reciprocal(st[:, 1, :], st[:, 3, :]).then_inc(n_rstd, 1)
                dve.wait_ge(n_rstd, n + 1)
                if not (peeled(i) and i == 0):
                    dve.wait_ge(stored[q], 16 * BT * l + i * 16)
                V.tensor_tensor(o_t[q][:, :, :], xc[:, :, :], st[:, 1, :].rearrange(bc, a=1).to_broadcast([P, NPP, D]),
                                ALU.mult).then_inc(finished, 1)

            for l in range(LAYERS):
                edge_pass(l)
                if l in GRU:
                    def body(i):
                        for q in range(2):
                            for g in range(2):
                                n = gru_base(l) + i * 4 + q * 2 + g
                                dve.wait_ge(g_transposed, n + 1)
                                V.tensor_copy(bT[g][:, :], psB[g][0:KB, :]).then_inc(bT_ready, 1)
                                dve.wait_ge(gates, n + 1)
                                V.tensor_tensor(d3_t[g][:, :, :], rz_t[g][:, :, 0:D], psG[g][:, :, 3 * D:GW],
                                                ALU.mult).then_inc(n_prod, 1)
                                dve.wait_ge(n_prod, n + 1)
                                V.tensor_tensor(d2_t[g][:, :, :], d3_t[g][:, :, :], psG[g][:, :, 2 * D:3 * D],
                                                ALU.add).then_inc(n_pre, 1)
                            if l in LN:
                                m = ln_base(l) + i * 2 + q
                                dve.wait_ge(g_new, gru_base(l) - TILES + (i * 4 + q * 2 + 2))
                                V.tensor_tensor(z_t[q][:, :, :], z_t[q][:, :, :], res_t[q][:, :, :], ALU.add
                                                ).then_inc(z_ready, 1)
                                dve.wait_ge(z_ready, m + 1)
                                layernorm(l, i, q)
                    walk(dve, BT, body)
                else:
                    w = {0: 0, 1: 1, 2: 2, 5: 3}[l]
                    bias_b = bias[w][:, :].rearrange("p (a d) -> p a d", a=1).to_broadcast([P, NPP, D])

                    def body(i):
                        for q in range(2):
                            n = gcn_base(l) + i * 2 + q
                            z = z_t[q]
                            dve.wait_ge(mm_done, n + 1)
                            V.tensor_tensor(z[:, :, :], psB[q][:, :].rearrange("p (j d) -> p j d", d=D), bias_b,
                                            ALU.add).then_inc(z_biased, 1)
                            if l == 0:
                                continue
                            m = ln_base(l) + i * 2 + q
                            dve.wait_ge(z_biased, n + 1)
                            if l == 1:
                                V.tensor_tensor(z[:, :, :], z[:, :, :], res_t[q][:, :, :], ALU.add
                                                ).then_inc(z_ready, 1)
                            elif l == 2:
                                V.scalar_tensor_tensor(y1_t[q][:, :, :], z[:, :, :], 0.1, z[:, :, :], ALU.mult,
                                                       ALU.max).then_inc(z_acted, 1)
                                dve.wait_ge(z_acted, i * 2 + q + 1)
                                V.tensor_tensor(z[:, :, :], y1_t[q][:, :, :], h_t[q][:, :, :], ALU.add
                                                ).then_inc(z_ready, 1)
                            else:
                                V.scalar_tensor_tensor(z[:, :, :], z[:, :, :], 0.0, h_t[q][:, :, :], ALU.max,
                                                       ALU.add).then_inc(z_ready, 1)
                            dve.wait_ge(z_ready, m + 1)
                            layernorm(l, i, q)
                    walk(dve, BT, body)

        @block.tensor
        def _(pe):
            pe.wait_ge(prep_t, 1)
            for b in range(CB):
                a = 1
                nc.tensor.transpose(psA[0][:, b * P:(b + 1) * P], first[a][:, b, :], ident[:, :])
                ins = nc.tensor.transpose(psA[1][:, b * P:(b + 1) * P], first[1 - a][:, b, :], ident[:, :])
            ins.then_inc(fold_mm, 1)
            for r in range(2):
                c = slice(r * 3 * D, (r + 1) * 3 * D)
                nc.tensor.matmul(psB[0][0:D, c], wms[r][:, :], wih[r][:, :], start=True, stop=True)
                ins = nc.tensor.matmul(psB[1][0:D + AW, c], wmd[r][:, :], wih[r][:, :], start=True, stop=True)
            ins.then_inc(fold_mm, 1)
            pe.wait_ge(ones_set, 1)
            pe.wait_ge(bias_rows, 32)
            pe.wait_ge(bw_loaded, 16 * 12)

            def edge_pass(p):
                src, w = (erows, AW) if p == "aux" else (rows, D)

                def body(i):
                    for q in range(2):
                        n = edge_base(p) + i
                        if p == "aux":
                            pe.wait_ge(e_loaded[q], (i + 1) * 16)
                        else:
                            pe.wait_ge(gathered[q], (gather_base(p) + i + 1) * (16 * GC))
                        pe.wait_ge(sel_built[q], n + 1)
                        if not (p == "aux" and peeled(i) and i == 0):
                            pe.wait_ge(sums_out[q], n)
                        ps = psG[q][:, :, :].rearrange("p a b -> p (a b)")
                        for c in range(GC):
                            ins = nc.tensor.matmul(ps[:, c * w:(c + 1) * w], sel[q][:, c, :], src[q][:, c, :],
                                                   start=True, stop=True)
                        ins.then_inc(combined[q], 1)
                walk(pe, HALF, body)
                pe.wait_ge(c_loaded, 32 * (carry_no(p) + 1))
                cb = cbuf_aux if p == "aux" else cbuf
                for b in range(CB):
                    for k in range(CB):
                        ins = nc.tensor.matmul(psB[0][:, b * w:(b + 1) * w], same[:, k, b * P:(b + 1) * P],
                                               cb[:, k, :], start=(k == 0), stop=(k == CB - 1))
                ins.then_inc(c_combined, 1)

            edge_pass("aux")
            for l in range(LAYERS):
                edge_pass(l)
                if l in GRU:
                    r = GRU.index(l)

                    def body(i):
                        for q in range(2):
                            pe.wait_ge(loaded[q], load_base(l) + (i + 1) * (16 * LOADS[l]))
                            pe.wait_ge(b_ready, 2 * TILES * r + (i * 4 + q * 2 + 2))
                            for g in range(2):
                                n = gru_base(l) + i * 4 + q * 2 + g
                                for j in range(HN):
                                    nc.tensor.transpose(psA[g][:, j * P:(j + 1) * P], ah_t[q][:, g * HN + j, :],
                                                        ident[:, :])
                                    ins = nc.tensor.transpose(psB[g][0:KB, j * P:(j + 1) * P],
                                                              b_t[q][:, g * HN + j, :], ident[:, :])
                                ins.then_inc(g_transposed, 1)
                                pe.wait_ge(aT_ready, n + 1)
                                pe.wait_ge(bT_ready, n + 1)
                                if not (peeled(i) and i == 0 and q == 0):
                                    pe.wait_ge(n_pre, n - 1)
                                for j in range(HN):
                                    nc.tensor.matmul(psG[g][:, j, :], aT[g][:, j * P:(j + 1) * P], RA[r][:, :],
                                                     start=True, stop=False)
                                    ins = nc.tensor.matmul(psG[g][:, j, :], bT[g][:, j * P:(j + 1) * P],
                                                           RB[r][:, :], start=False, stop=True)
                                ins.then_inc(g_mm, 1)
                    walk(pe, BT, body)
                else:
                    w = {0: 0, 1: 1, 2: 2, 5: 3}[l]

                    def body(i):
                        for q in range(2):
                            n = gcn_base(l) + i * 2 + q
                            pe.wait_ge(y_ready, n + 1)
                            for j in range(NPP // 2):
                                ins = nc.tensor.transpose(psA[q][:, j * P:(j + 1) * P],
                                                          y_t[q][:, 2 * j:2 * j + 2, :].rearrange("p a d -> p (a d)"),
                                                          ident[:, :])
                            ins.then_inc(y_transposed, 1)
                            pe.wait_ge(yT_ready, n + 1)
                            if not (peeled(i) and i == 0):
                                pe.wait_ge(z_biased, n - 1)
                            for j in range(NPP // 2):
                                ins = nc.tensor.matmul(psB[q][:, j * P:(j + 1) * P], yT[q][:, j * P:(j + 1) * P],
                                                       BW[w][:, :], start=True, stop=True)
                            ins.then_inc(mm_done, 1)
                    walk(pe, BT, body)


def kernel(**inputs):
    import numpy as np
    import concourse.bacc as bacc
    from concourse.bass_utils import run_bass_kernel_spmd as run

    g = {k: np.asarray(v) for k, v in inputs.items()}
    pad = CB * P * P
    src = np.concatenate([g["src"], np.zeros(CHUNKS * P - E, np.int32)])
    dst = np.concatenate([g["dst"], np.full(pad - E, N, np.int32)])
    before = np.concatenate([np.full(P + 1, -1, np.int32), dst])

    def by_chunk(a):
        return a.reshape(CB, P, P).transpose(1, 0, 2).reshape(P, CB * P)

    arrays = {
        "x": g["x"],
        "edges": np.concatenate([g["edge_attr_16"], np.zeros((CHUNKS * P - E, DE), np.float32)]),
        "src_cols": src.reshape(CHUNKS, P).T,
        "dst_rows": by_chunk(dst),
        "prev_rows": by_chunk(before[P:P + pad]),
        "back": before[0:pad:P].reshape(CB, P).T,
        "head": np.broadcast_to(dst[0:pad:P], (P, CB * P)),
    }
    for l, (w, b) in enumerate([(g["L0_gnn_W1"].T, "L0_gnn_b1"), (g["L0_gnn_W2"].T, "L0_gnn_b2"),
                                (g["L1_gnn_weight"], "L1_gnn_bias"), (g["L3_gnn_W"].T, "L3_gnn_b")]):
        arrays[f"w{l}"] = w
        arrays[f"bias{l}"] = np.broadcast_to(g[b], (P, D))
    zero = np.zeros(D, np.float32)
    for r in range(2):
        wm, bm = g["L2_gnn_W_msg"][r], g["L2_gnn_b_msg"][r]
        arrays[f"wms{r}"] = wm[D:2 * D].T
        arrays[f"wmd{r}"] = np.concatenate([wm[0:D], wm[2 * D:], bm[None]]).T
        arrays[f"wih{r}"] = g["L2_gnn_W_ih"][r].T
        arrays[f"whh{r}"] = g["L2_gnn_W_hh"][r].T
        bi, bh = g["L2_gnn_b_ih"][r], g["L2_gnn_b_hh"][r]
        arrays[f"gbias{r}"] = np.stack([np.concatenate([bi, zero]), np.concatenate([bh[:2 * D], zero, bh[2 * D:]])])

    nc = bacc.Bacc("TRN2", target_bir_lowering=False, num_devices=1)
    feed, aps = {}, {}
    for name, a in arrays.items():
        feed[f"{name}_dram"] = np.ascontiguousarray(a)
        aps[name] = nc.dram_tensor(f"{name}_dram", a.shape, mybir.dt.from_np(a.dtype), kind="ExternalInput").ap()
    aps["out"] = nc.dram_tensor("out_dram", (N, D), mybir.dt.float32, kind="ExternalOutput").ap()
    build(nc, aps)
    r = run(nc, [feed], core_ids=[0])
    return r.results[0]["out_dram"]
```

```python
import concourse.bass as bass
from concourse import mybir
from contextlib import ExitStack

N = 100000
E = 50000
D = 64
DE = 16
P = 128
NPP = 8
TILE = P * NPP
TILES = -(-N // TILE)
NPAD = TILES * TILE
LASTP = (N - (TILES - 1) * TILE) // NPP
GC = 7
HALF = -(-E // (P * GC * 2))
GROUPS = 2 * HALF
CHUNKS = GROUPS * GC
CB = -(-CHUNKS // P)
LASTC = CHUNKS - (CB - 1) * P
AW = DE + 1
KB = D + AW + 2
GW = 4 * D
FAR = float(1 << 20)
EPS = 1e-5
LAYERS = 6
GRU = (3, 4)
LN = (1, 2, 4, 5)
LOADS = (3, 4, 3, 3, 4, 3)
LAG = (2, 2, 2, 0, 1, 2)
SLOTS = 4
NEWTON = 12
UNITS = 2 * TILES
HN = NPP // 2


def build(nc, t):
    f32, i32 = mybir.dt.float32, mybir.dt.int32
    ALU, ACT, AX = mybir.AluOpType, mybir.ActivationFunctionType, mybir.AxisListType
    with ExitStack() as ctx:
        def sb(name, shape, dt=f32):
            return ctx.enter_context(nc.sbuf_tensor(name, shape, dt))

        def two(name, shape, dt=f32):
            return [sb(f"{name}{q}", shape, dt) for q in range(2)]

        def sem(name):
            return ctx.enter_context(nc.semaphore(name))

        def sems(name):
            return [sem(f"{name}{q}") for q in range(2)]

        def dram(name, shape):
            return nc.dram_tensor(name, shape, f32).ap()

        agg = dram("agg", (NPAD, D))
        aux = dram("aux", (NPAD, AW))
        carry = dram("carry", (CHUNKS, D))
        carry_aux = dram("carry_aux", (CHUNKS, AW))
        s_tab = dram("s_tab", (NPAD, 1))
        h1, x1, x2, v1, x3 = (dram(n, (NPAD, D)) for n in ("h1", "x1", "x2", "v1", "x3"))
        layer_in = [t["x"], h1, x1, x2, v1, x3]
        layer_res = [None, t["x"], None, None, x2, None]
        layer_out = [h1, x1, x2, v1, x3, t["out"]]

        lane_i = sb("lane_i", [P, P], i32)
        lane = sb("lane", [P, P])
        part_i = sb("part_i", [P, 1], i32)
        part = sb("part", [P, 1])
        ident = sb("ident", [P, P])
        src_c = sb("src_c", [P, CHUNKS], i32)
        dst_r = sb("dst_r", [P, CB * P], i32)
        prv_r = sb("prv_r", [P, CB * P], i32)
        back_r = sb("back_r", [P, CB], i32)
        head_r = sb("head_r", [P, CB * P], i32)
        dstf = sb("dstf", [P, CB, P])
        prvf = sb("prvf", [P, CB, P])
        backf = sb("backf", [P, CB])
        headf = sb("headf", [P, CB * P])
        begin = sb("begin", [P, CB, P])
        first = two("first", [P, CB, P])
        sidx_r = sb("sidx_r", [P, CB, P])
        first_c = sb("first_c", [P, CB * P])
        dst_idx = sb("dst_idx", [P, CB * P], i32)
        cont = sb("cont", [P, CB])
        lead = sb("lead", [P, CB])
        cidx_f = sb("cidx_f", [P, CB])
        carry_src = sb("carry_src", [P, CB], i32)
        carry_dst = sb("carry_dst", [P, CB], i32)
        same = sb("same", [P, CB, CB * P])
        edge_w = sb("edge_w", [P, CHUNKS])
        deg = sb("deg", [P, NPAD // P])
        eps = sb("eps", [P, 1])
        s_big = sb("s_big", [P, NPAD // P])
        WB = NPAD // P // 8
        wide = sb("wide", [P, WB * D])
        BW = [sb(f"bw{l}", [P, P]) for l in range(4)]
        bias = [sb(f"bias{l}", [P, D]) for l in range(4)]
        wms = [sb(f"wms{r}", [P, D]) for r in range(2)]
        wmd = [sb(f"wmd{r}", [P, D + AW]) for r in range(2)]
        wih = [sb(f"wih{r}", [P, 3 * D]) for r in range(2)]
        RA = [sb(f"ra{r}", [P, GW]) for r in range(2)]
        RB = [sb(f"rb{r}", [KB, GW]) for r in range(2)]

        src_st = two("src_st", [P, GC], i32)
        dst_st = two("dst_st", [P, GC], i32)
        rows = two("rows", [P, GC, D])
        erows = two("erows", [P, GC, AW])
        w_st = two("w_st", [P, GC])
        sel = two("sel", [P, GC, P])
        sums = two("sums", [P, GC, D])
        esums = two("esums", [P, GC, AW])
        cbuf = sb("cbuf", [P, CB, D])
        cbuf_aux = sb("cbuf_aux", [P, CB, AW])
        cold = sb("cold", [P, CB, D])
        cold_aux = sb("cold_aux", [P, CB, AW])
        cnew = sb("cnew", [P, CB, D])
        cnew_aux = sb("cnew_aux", [P, CB, AW])

        h_t = [sb(f"h_t{r}", [P, NPP, D]) for r in range(SLOTS)]
        agg_t = [sb(f"agg_t{r}", [P, NPP, D]) for r in range(SLOTS)]
        res_t = [sb(f"res_t{r}", [P, NPP, D]) for r in range(SLOTS)]
        s_t = [sb(f"s_t{r}", [P, NPP]) for r in range(SLOTS)]
        aux_t = [sb(f"aux_t{r}", [P, NPP, AW]) for r in range(SLOTS)]
        y_t = two("y_t", [P, NPP, D])
        y0_t = two("y0_t", [P, NPP, D])
        y1_t = two("y1_t", [P, NPP, D])
        za_t = two("za_t", [P, NPP, D])
        yT = two("yT", [P, NPP * D])
        z_t = two("z_t", [P, NPP, D])
        xc_t = two("xc_t", [P, NPP, D])
        sq_t = two("sq_t", [P, NPP, D])
        o_t = two("o_t", [P, NPP, D])
        st_t = two("st_t", [P, 6, NPP])
        ah_t = [sb(f"ah_t{r}", [P, NPP, 2 * D]) for r in range(SLOTS)]
        b_t = two("b_t", [P, NPP, KB])
        aT = two("aT", [P, HN * P])
        bT = two("bT", [KB, HN * P])
        rz_t = two("rz_t", [P, HN, 2 * D])
        n_t = two("n_t", [P, HN, D])
        m_t = two("m_t", [P, HN, D])
        d_t = two("d_t", [P, HN, D])
        d2_t = two("d2_t", [P, HN, D])
        d3_t = two("d3_t", [P, HN, D])

        psA = [ctx.enter_context(nc.psum_tensor(f"psA{q}", [P, 512], f32)) for q in range(2)]
        psB = [ctx.enter_context(nc.psum_tensor(f"psB{q}", [P, 512], f32)) for q in range(2)]
        psG = [ctx.enter_context(nc.psum_tensor(f"psG{q}", [P, HN, GW], f32)) for q in range(2)]

        in_loaded = sem("in_loaded")
        bw_zeroed = sem("bw_zeroed")
        bw_loaded = sem("bw_loaded")
        zeros_set = sem("zeros_set")
        tabs_zeroed = sem("tabs_zeroed")
        iotas = sem("iotas")
        prep = sem("prep")
        prep_t = sem("prep_t")
        prep_w = sem("prep_w")
        fold_mm = sem("fold_mm")
        ones_set = sem("ones_set")
        bias_rows = sem("bias_rows")
        aux_loaded = sem("aux_loaded")
        s_done = sem("s_done")
        deg_root = sem("deg_root")
        s_ready = sem("s_ready")
        eps_set = sem("eps_set")
        s_stored = sem("s_stored")
        src_staged, dst_staged = sems("src_staged"), sems("dst_staged")
        gathered, e_loaded = sems("gathered"), sems("e_loaded")
        w_copied, sel_built = sems("w_copied"), sems("sel_built")
        combined, sums_out = sems("combined"), sems("sums_out")
        scattered, carried = sems("scattered"), sems("carried")
        pool_turn = sem("pool_turn")
        c_loaded, c_combined, c_gathered = sem("c_loaded"), sem("c_combined"), sem("c_gathered")
        c_added, c_scattered = sem("c_added"), sem("c_scattered")
        loaded, stored = [sem(f"loaded{r}") for r in range(SLOTS)], sems("stored")
        newton = sem("newton")
        finished = sem("finished")
        y_scaled, y_summed, y_ready = sem("y_scaled"), sem("y_summed"), sem("y_ready")
        y_transposed, yT_ready, mm_done = sem("y_transposed"), sem("yT_ready"), sem("mm_done")
        z_biased, z_acted, z_ready = sem("z_biased"), sem("z_acted"), sem("z_ready")
        n_sum, n_mean, n_centred = sem("n_sum"), sem("n_mean"), sem("n_centred")
        n_squared, n_var, n_std, n_rstd = sem("n_squared"), sem("n_var"), sem("n_std"), sem("n_rstd")
        b_ready, g_transposed = sem("b_ready"), sem("g_transposed")
        aT_ready, bT_ready, g_mm = sem("aT_ready"), sem("bT_ready"), sem("g_mm")
        gates, n_prod, n_pre, n_act = sem("gates"), sem("n_prod"), sem("n_pre"), sem("n_act")
        g_diff, g_scaled, g_new = sem("g_diff"), sem("g_scaled"), sem("g_new")

        def edge_base(p):
            return 0 if p == "aux" else HALF * (1 + p)

        def gather_base(p):
            return 0 if p == "w" else HALF * (1 + p)

        def carry_no(p):
            return 0 if p == "aux" else 1 + p

        def gcn_base(l):
            return TILES * sum(k not in GRU for k in range(l))

        def ln_base(l):
            return TILES * sum(k in LN for k in range(l))

        def n_std_base(l):
            return TILES * sum(k in LN and k not in GRU for k in range(l))

        def gru_base(l):
            return UNITS * sum(k in GRU for k in range(l))

        def load_base(l, r):
            return 16 * (-(-(TILES - r) // SLOTS)) * sum(LOADS[:l])

        def walk(eng, n, body):
            body(0)
            with eng.Fori(1, n - 1) as i:
                body(i)
            body(n - 1)

        def peeled(i):
            return isinstance(i, int)

        class Tile:
            def __init__(self, step, k):
                self.no = step * SLOTS + k
                self.step, self.r, self.q = step, k, k % 2
                self.pair = step * 2 + k // 2
                self.there = not peeled(step) or 0 <= self.no < TILES
                self.early = peeled(step) and self.no < 2

        class Unit:
            def __init__(self, step, k):
                self.tile = Tile(step, k // 2)
                self.g = k % 2
                self.no = step * (2 * SLOTS) + k
                self.there = self.tile.there
                self.early = peeled(step) and self.no < 2

        def tile_at(i, k, lag):
            return Tile(i + (k - lag) // SLOTS, (k - lag) % SLOTS)

        def unit_at(i, k, lag):
            return Unit(i + (k - lag) // (2 * SLOTS), (k - lag) % (2 * SLOTS))

        def pipeline(eng, body, lag, stop=TILES // SLOTS):
            lead = -(-lag // SLOTS)
            for i in range(lead):
                body(i)
            with eng.Fori(lead, stop) as i:
                body(i)
            for i in range(stop, -(-(TILES + lag) // SLOTS)):
                body(i)

        BT = TILES // 2
        in_names = ("src_cols", "dst_rows", "prev_rows", "back", "head")
        PREP_LOADS = len(in_names) + 4 + 2 * 3
        C_ROWS = CB

        block = ctx.enter_context(nc.Block())

        @block.sync
        def _(sp):
            for name, buf in zip(in_names, (src_c, dst_r, prv_r, back_r, head_r)):
                sp.dma_start(buf[:, :], t[name]).then_inc(in_loaded, 16)
            for l in range(4):
                sp.dma_start(bias[l][:, :], t[f"bias{l}"]).then_inc(in_loaded, 16)
            for r in range(2):
                sp.dma_start(wms[r][:, :], t[f"wms{r}"]).then_inc(in_loaded, 16)
                sp.dma_start(wmd[r][:, :], t[f"wmd{r}"]).then_inc(in_loaded, 16)
                sp.dma_start(wih[r][:, :], t[f"wih{r}"]).then_inc(in_loaded, 16)
            sp.wait_ge(bw_zeroed, 1)
            for l in range(4):
                sp.dma_start(BW[l][0:D, 0:D], t[f"w{l}"]).then_inc(bw_loaded, 16)
                sp.dma_start(BW[l][D:P, D:P], t[f"w{l}"]).then_inc(bw_loaded, 16)
            for r in range(2):
                sp.dma_start(RA[r][D:P, 0:2 * D], t[f"whh{r}"][:, 0:2 * D]).then_inc(bw_loaded, 16)
                sp.dma_start(RA[r][D:P, 3 * D:GW], t[f"whh{r}"][:, 2 * D:3 * D]).then_inc(bw_loaded, 16)
            sp.wait_ge(zeros_set, 1)
            for k in range(8):
                sp.dma_start(agg.rearrange("(p k) d -> p (k d)", p=P)[:, k * WB * D:(k + 1) * WB * D],
                             wide[:, :]).then_inc(tabs_zeroed, 16)
            for k in range(8):
                sp.dma_start(aux.rearrange("(p k) d -> p (k d)", p=P)[:, k * WB * AW:(k + 1) * WB * AW],
                             wide[:, 0:WB * AW]).then_inc(tabs_zeroed, 16)
            sp.wait_ge(ones_set, 1)
            for r in range(2):
                sp.dma_start(RB[r][KB - 2:KB, :], t[f"gbias{r}"]).then_inc(bias_rows, 16)

            def edge_pass(p):
                out, table, w = (esums, carry_aux, AW) if p == "aux" else (sums, carry, D)

                def body(i):
                    for q in range(2):
                        n = edge_base(p) + i
                        if p == "aux":
                            if not (peeled(i) and i == 0):
                                sp.wait_ge(combined[q], n)
                            e0 = (i * 2 + q) * (GC * P)
                            sp.dma_start(erows[q][:, :, 0:DE], t["edges"][bass.ds(e0, GC * P), :]
                                         .rearrange("(c p) d -> p c d", p=P)).then_inc(e_loaded[q], 16)
                    for q in range(2):
                        n = edge_base(p) + i
                        sp.wait_ge(sums_out[q], n + 1)
                        sp.dma_start(table[bass.ds((i * 2 + q) * GC, GC), :].rearrange("(a c) d -> a c d", a=1),
                                     out[q][0:1, :, :]).then_inc(carried[q], 16)
                walk(sp, HALF, body)
                for q in range(2):
                    sp.wait_ge(carried[q], 16 * (edge_base(p) + HALF))
                dst = cbuf_aux if p == "aux" else cbuf
                full = (CB - 1) * P
                sp.dma_start(dst[:, 0:CB - 1, :], table[0:full, :].rearrange("(b p) d -> p b d", p=P)
                             ).then_inc(c_loaded, 16)
                sp.dma_start(dst[0:LASTC, CB - 1, :], table[full:CHUNKS, :]).then_inc(c_loaded, 16)

            edge_pass("aux")
            sp.wait_ge(c_scattered, 16 * C_ROWS)
            av = aux.rearrange("(p k) d -> p (k d)", p=P)
            for k in range(8):
                if k:
                    sp.wait_ge(s_done, k)
                sp.dma_start(wide[:, 0:WB * AW], av[:, k * WB * AW:(k + 1) * WB * AW]).then_inc(aux_loaded, 16)
            sp.wait_ge(s_ready, 1)
            sp.dma_start(s_tab.rearrange("(p k) a -> p (k a)", p=P), s_big[:, :]).then_inc(s_stored, 16)

            for l in range(LAYERS):
                edge_pass(l)
                sp.wait_ge(c_scattered, 16 * C_ROWS * (carry_no(l) + 1))

                def view(tab, tile, parts=P):
                    r = tile * TILE
                    return tab[bass.ds(r, parts * NPP), :].rearrange("(p j) d -> p j d", p=parts)

                def load(tile, q):
                    parts = LASTP if peeled(tile) and tile == TILES - 1 and l == 0 else P
                    if l in GRU:
                        sp.dma_start(ah_t[q][:, :, 0:D], view(agg, tile)).then_inc(loaded[q], 16)
                        sp.dma_start(ah_t[q][:, :, D:2 * D], view(layer_in[l], tile)).then_inc(loaded[q], 16)
                        sp.dma_start(aux_t[q][:, :, :], view(aux, tile)).then_inc(loaded[q], 16)
                    else:
                        sp.dma_start(agg_t[q][:, :, :], view(agg, tile)).then_inc(loaded[q], 16)
                        sp.dma_start(h_t[q][0:parts, :, :], view(layer_in[l], tile, parts)).then_inc(loaded[q], 16)
                        sp.dma_start(s_t[q][:, :], s_tab[bass.ds(tile * TILE, TILE), :]
                                     .rearrange("(p j) a -> p (j a)", p=P)).then_inc(loaded[q], 16)
                    if layer_res[l] is not None:
                        parts = LASTP if peeled(tile) and tile == TILES - 1 and l == 1 else P
                        sp.dma_start(res_t[q][0:parts, :, :], view(layer_res[l], tile, parts)).then_inc(loaded[q], 16)

                def store(tile, q):
                    parts = LASTP if peeled(tile) and tile == TILES - 1 and l == LAYERS - 1 else P
                    sp.dma_start(view(layer_out[l], tile, parts), o_t[q][0:parts, :, :]).then_inc(stored[q], 16)

                for r in range(SLOTS):
                    load(r, r)

                def body(i):
                    for k in range(SLOTS):
                        a, b = tile_at(i, k, 0), tile_at(i, k, LAG[l])
                        if a.there:
                            if l == 0:
                                sp.wait_ge(y_ready, gcn_base(l) + a.no + 1)
                            elif l == 3:
                                sp.wait_ge(g_new, gru_base(l) + a.no * 2 + 2)
                            else:
                                sp.wait_ge(z_ready, ln_base(l) + a.no + 1)
                            if not (peeled(i) and a.no + SLOTS >= TILES):
                                load(a.no + SLOTS, k)
                        if b.there:
                            sp.wait_ge(finished, TILES * l + b.no + 1)
                            store(b.no, b.q)
                pipeline(sp, body, LAG[l], stop=TILES // SLOTS - 1)
                for q in range(2):
                    sp.wait_ge(stored[q], 16 * BT * (l + 1))

        @block.gpsimd
        def _(pool):
            nc.gpsimd.iota(lane_i[:, :], pattern=[[1, P]], base=0, channel_multiplier=0).then_inc(iotas, 1)
            nc.gpsimd.iota(part_i[:, :], pattern=[[0, 1]], base=0, channel_multiplier=1).then_inc(iotas, 1)
            for q in range(2):
                nc.gpsimd.memset(b_t[q][:, :, :], 1.0).then_inc(iotas, 1)
            for b in (h_t[(TILES - 1) % SLOTS], res_t[(TILES - 1) % SLOTS]):
                nc.gpsimd.memset(b[:, :, :], 0.0).then_inc(iotas, 1)
            pool.wait_ge(prep, 1)

            def gather_group(p, q, n):
                pool.wait_ge(src_staged[q], n + 1)
                pool.sem_inc(pool_turn, 1)
                tab = s_tab if p == "w" else layer_in[p]
                for c in range(GC):
                    dst = w_st[q][:, c:c + 1] if p == "w" else rows[q][:, c, :]
                    nc.gpsimd.indirect_dma_start(dst, None, tab, bass.IndirectOffsetOnAxis(
                        ap=src_st[q][:, c:c + 1], axis=0)).then_inc(gathered[q], 16)

            def scatter_group(p, q, i):
                out, tab = (esums, aux) if p == "aux" else (sums, agg)
                n = edge_base(p) + i
                pool.wait_ge(dst_staged[q], n + 1)
                pool.wait_ge(sums_out[q], n + 1)
                pool.sem_inc(pool_turn, 1)
                for c in range(GC):
                    nc.gpsimd.indirect_dma_start(tab, bass.IndirectOffsetOnAxis(
                        ap=dst_st[q][:, c:c + 1], axis=0), out[q][:, c, :], None,
                        bounds_check=N - 1, oob_is_err=False).then_inc(scattered[q], 16)

            def carry_stage(p):
                old, new, tab = (cold_aux, cnew_aux, aux) if p == "aux" else (cold, cnew, agg)
                for q in range(2):
                    pool.wait_ge(scattered[q], 16 * GC * (edge_base(p) + HALF))
                for b in range(CB):
                    nc.gpsimd.indirect_dma_start(old[:, b, :], None, tab, bass.IndirectOffsetOnAxis(
                        ap=carry_src[:, b:b + 1], axis=0), bounds_check=N - 1, oob_is_err=False
                        ).then_inc(c_gathered, 16)
                pool.wait_ge(c_added, carry_no(p) + 1)
                for b in range(CB):
                    nc.gpsimd.indirect_dma_start(tab, bass.IndirectOffsetOnAxis(
                        ap=carry_dst[:, b:b + 1], axis=0), new[:, b, :], None,
                        bounds_check=N - 1, oob_is_err=False).then_inc(c_scattered, 16)

            pool.wait_ge(tabs_zeroed, 16 * 16)
            walk(pool, HALF, lambda i: [scatter_group("aux", q, i) for q in range(2)])
            carry_stage("aux")

            pool.wait_ge(s_stored, 16)
            walk(pool, HALF, lambda i: [gather_group("w", q, gather_base("w") + i) for q in range(2)])

            for l in range(LAYERS):
                if l:
                    for q in range(2):
                        pool.wait_ge(stored[q], 16 * BT * l)
                for q in range(2):
                    gather_group(l, q, gather_base(l))

                def body(i):
                    for q in range(2):
                        scatter_group(l, q, i)
                        if not (peeled(i) and i == HALF - 1):
                            gather_group(l, q, gather_base(l) + i + 1)
                walk(pool, HALF, body)
                carry_stage(l)

                if l in GRU:
                    def operand(a):
                        q = a.q
                        pool.wait_ge(loaded[a.r], load_base(l, a.r) + (a.step + 1) * (16 * LOADS[l]))
                        if not a.early:
                            pool.wait_ge(g_transposed, gru_base(l) + a.no * 2 - 2)
                        nc.gpsimd.tensor_tensor(b_t[q][:, :, 0:D], ah_t[a.r][:, :, D:2 * D],
                                                aux_t[a.r][:, :, DE:AW].to_broadcast([P, NPP, D]),
                                                ALU.mult).then_inc(b_ready, 1)
                        nc.gpsimd.tensor_copy(b_t[q][:, :, D:D + AW], aux_t[a.r][:, :, :]).then_inc(b_ready, 1)

                    def new_state(u):
                        n, g, q = gru_base(l) + u.no, u.g, u.tile.q
                        half = slice(g * HN, (g + 1) * HN)
                        out = z_t if l in LN else o_t
                        pool.wait_ge(n_act, n + 1)
                        nc.gpsimd.tensor_tensor(d_t[g][:, :, :], ah_t[u.tile.r][:, half, D:2 * D], n_t[g][:, :, :],
                                                ALU.subtract).then_inc(g_diff, 1)
                        pool.wait_ge(g_diff, n + 1)
                        nc.gpsimd.tensor_tensor(m_t[g][:, :, :], d_t[g][:, :, :], rz_t[g][:, :, D:2 * D],
                                                ALU.mult).then_inc(g_scaled, 1)
                        if g == 0 and not u.tile.early:
                            if l in LN:
                                pool.wait_ge(n_centred, ln_base(l) + u.tile.no - 1)
                            else:
                                pool.wait_ge(stored[q], 16 * BT * l + u.tile.pair * 16)
                        pool.wait_ge(g_scaled, n + 1)
                        ins = nc.gpsimd.tensor_tensor(out[q][:, half, :], m_t[g][:, :, :], n_t[g][:, :, :], ALU.add)
                        ins.then_inc(g_new, 1)
                        if l not in LN and g == 1:
                            pool.wait_ge(g_new, n + 1)
                            pool.sem_inc(finished, 1)

                    operand(Tile(0, 0))

                    def body(i):
                        for k in range(2 * SLOTS):
                            if k % 2 == 0:
                                a = tile_at(i, k // 2, -1)
                                if a.there:
                                    operand(a)
                            u = unit_at(i, k, 2)
                            if u.there:
                                new_state(u)
                    pipeline(pool, body, 1)
                else:
                    def body(i):
                        for k in range(SLOTS):
                            a = tile_at(i, k, 0)
                            if not a.there:
                                continue
                            n, q, r = gcn_base(l) + a.no, a.q, a.r
                            pool.wait_ge(loaded[r], load_base(l, r) + (a.step + 1) * (16 * LOADS[l]))
                            s_b = s_t[r][:, :].rearrange("p (j a) -> p j a", a=1).to_broadcast([P, NPP, D])
                            nc.gpsimd.tensor_tensor(y0_t[q][:, :, :], h_t[r][:, :, :], s_b, ALU.mult
                                                    ).then_inc(y_scaled, 1)
                            pool.wait_ge(y_scaled, n + 1)
                            nc.gpsimd.tensor_tensor(y1_t[q][:, :, :], y0_t[q][:, :, :], agg_t[r][:, :, :], ALU.add
                                                    ).then_inc(y_summed, 1)
                            if not a.early:
                                pool.wait_ge(y_transposed, n - 1)
                            pool.wait_ge(y_summed, n + 1)
                            nc.gpsimd.tensor_tensor(y_t[q][:, :, :], y1_t[q][:, :, :], s_b, ALU.mult
                                                    ).then_inc(y_ready, 1)
                    pipeline(pool, body, 1)

        @block.scalar
        def _(act):
            def edge_pass(p):
                out, w = (esums, AW) if p == "aux" else (sums, D)

                def body(i):
                    for q in range(2):
                        n = edge_base(p) + i
                        if not (p == "aux" and peeled(i) and i == 0):
                            act.wait_ge(scattered[q], n * (16 * GC))
                            act.wait_ge(carried[q], n * 16)
                        act.wait_ge(combined[q], n + 1)
                        nc.scalar.copy(out[q][:, :, :], psG[q][:, :, :].rearrange("p a b -> p (a b)")[:, 0:GC * w]
                                       .rearrange("p (c d) -> p c d", d=w)).then_inc(sums_out[q], 1)
                walk(act, HALF, body)

            edge_pass("aux")
            act.wait_ge(eps_set, 1)
            act.wait_ge(s_done, 8)
            nc.scalar.activation(deg[:, :], deg[:, :], ACT.Sqrt).then_inc(deg_root, 1)
            for l in range(LAYERS):
                edge_pass(l)

                def square(a):
                    if a.there:
                        n = ln_base(l) + a.no
                        act.wait_ge(n_centred, n + 1)
                        if not a.early:
                            act.wait_ge(n_var, n - 1)
                        nc.scalar.activation(sq_t[a.q][:, :, :], xc_t[a.q][:, :, :], ACT.Square
                                             ).then_inc(n_squared, 1)

                def root(a):
                    if a.there:
                        n = ln_base(l) + a.no
                        act.wait_ge(n_var, n + 1)
                        nc.scalar.activation(st_t[a.q][:, 3, :], st_t[a.q][:, 2, :], ACT.Sqrt,
                                             bias=eps[:, 0:1], scale=1.0 / D).then_inc(n_std, 1)

                if l in GRU:
                    def body(i):
                        for k in range(2 * SLOTS):
                            u = unit_at(i, k, 0)
                            if u.there:
                                act.wait_ge(g_transposed, gru_base(l) + u.no + 1)
                                if not u.early:
                                    act.wait_ge(g_mm, gru_base(l) + u.no - 1)
                                nc.scalar.copy(aT[u.g][:, :], psA[u.g][:, :]).then_inc(aT_ready, 1)
                            u = unit_at(i, k, 1)
                            if u.there:
                                act.wait_ge(g_mm, gru_base(l) + u.no + 1)
                                if not u.early:
                                    act.wait_ge(g_scaled, gru_base(l) + u.no - 1)
                                nc.scalar.activation(rz_t[u.g][:, :, :], psG[u.g][:, :, 0:2 * D], ACT.Sigmoid
                                                     ).then_inc(gates, 1)
                            u = unit_at(i, k, 2)
                            if u.there:
                                act.wait_ge(n_pre, gru_base(l) + u.no + 1)
                                if not u.early:
                                    act.wait_ge(g_new, gru_base(l) + u.no - 1)
                                nc.scalar.activation(n_t[u.g][:, :, :], d2_t[u.g][:, :, :], ACT.Tanh
                                                     ).then_inc(n_act, 1)
                            if l in LN and k % 2 == 1:
                                square(tile_at(i, k // 2, 2))
                    pipeline(act, body, 3)
                else:
                    def body(i):
                        for k in range(SLOTS):
                            a = tile_at(i, k, 0)
                            if a.there:
                                act.wait_ge(y_transposed, gcn_base(l) + a.no + 1)
                                if not a.early:
                                    act.wait_ge(mm_done, gcn_base(l) + a.no - 1)
                                nc.scalar.copy(yT[a.q][:, :], psA[a.q][:, :]).then_inc(yT_ready, 1)
                            if l == 0:
                                a = tile_at(i, k, 1)
                                if a.there:
                                    if not a.early:
                                        act.wait_ge(stored[a.q], a.pair * 16)
                                    act.wait_ge(z_biased, gcn_base(l) + a.no + 1)
                                    nc.scalar.activation(o_t[a.q][:, :, :], z_t[a.q][:, :, :], ACT.Relu
                                                         ).then_inc(finished, 1)
                            else:
                                square(tile_at(i, k, 1))
                                root(tile_at(i, k, 2))
                    pipeline(act, body, 2)

        @block.vector
        def _(dve):
            V = nc.vector
            for l in range(4):
                ins = V.memset(BW[l][:, :], 0.0)
            for r in range(2):
                ins = V.memset(RA[r][:, :], 0.0)
            ins.then_inc(bw_zeroed, 1)
            V.memset(wide[:, :], 0.0).then_inc(zeros_set, 1)
            V.memset(eps[:, :], EPS).then_inc(eps_set, 1)
            V.memset(cbuf[:, :, :], 0.0)
            V.memset(cbuf_aux[:, :, :], 0.0)
            V.memset(cold[:, :, :], 0.0)
            V.memset(cold_aux[:, :, :], 0.0)
            for r in range(2):
                V.memset(RB[r][:, :], 0.0)
            for q in range(2):
                V.memset(erows[q][:, :, :], 1.0)
            steps = [0]

            def link(ins):
                steps[0] += 1
                ins.then_inc(prep_w, 1)
                dve.wait_ge(prep_w, steps[0])

            dve.wait_ge(iotas, 6)
            V.tensor_copy(lane[:, :], lane_i[:, :])
            link(V.tensor_copy(part[:, :], part_i[:, :]))
            V.tensor_scalar(ident[:, :], lane[:, :], part[:, 0:1], None, ALU.is_equal)
            dve.wait_ge(in_loaded, 16 * PREP_LOADS)
            flat = "p a b -> p (a b)"
            V.tensor_copy(dstf[:, :, :].rearrange(flat), dst_r[:, :])
            V.tensor_copy(prvf[:, :, :].rearrange(flat), prv_r[:, :])
            V.tensor_copy(backf[:, :], back_r[:, :])
            link(V.tensor_copy(headf[:, :], head_r[:, :]))
            link(V.tensor_tensor(begin[:, :, :], dstf[:, :, :], prvf[:, :, :], ALU.not_equal))
            lanes = lane[:, :].rearrange("p (a l) -> p a l", a=1).to_broadcast([P, CB, P])
            link(V.tensor_tensor(first[0][:, :, :], begin[:, :, :], lanes, ALU.mult))
            k, a = 1, 0
            while k < P:
                V.tensor_copy(first[1 - a][:, :, 0:k], first[a][:, :, 0:k])
                link(V.tensor_tensor(first[1 - a][:, :, k:P], first[a][:, :, k:P], first[a][:, :, 0:P - k], ALU.max))
                k, a = 2 * k, 1 - a
            link(V.tensor_scalar(sidx_r[:, :, :], begin[:, :, :], -FAR, FAR, ALU.mult, ALU.add))
            link(V.tensor_tensor(first[1 - a][:, :, :], sidx_r[:, :, :], dstf[:, :, :], ALU.add))
            link(V.tensor_scalar(cont[:, :], begin[:, :, 0], -1.0, 1.0, ALU.mult, ALU.add))
            link(V.tensor_tensor(lead[:, :], backf[:, :], dstf[:, :, 0], ALU.not_equal))
            link(V.tensor_tensor(cidx_f[:, :], lead[:, :], cont[:, :], ALU.mult))
            link(V.tensor_scalar(lead[:, :], cidx_f[:, :], -FAR, FAR, ALU.mult, ALU.add))
            link(V.tensor_tensor(cidx_f[:, :], lead[:, :], dstf[:, :, 0], ALU.add))
            V.tensor_copy(carry_dst[:, :], cidx_f[:, :])
            V.tensor_copy(carry_src[:, :], dstf[:, :, 0])
            for b in range(CB):
                ins = V.tensor_scalar(same[:, b, :], headf[:, :], dstf[:, b, 0:1], cont[:, b:b + 1], ALU.is_equal,
                                      ALU.mult)
            ins.then_inc(prep_t, 1)
            dve.wait_ge(fold_mm, 1)
            V.tensor_copy(first_c[:, :], psA[0][:, :])
            V.tensor_copy(dst_idx[:, :], psA[1][:, :]).then_inc(prep, 1)
            dve.wait_ge(prep, 1)
            dve.wait_ge(fold_mm, 2)
            for r in range(2):
                V.tensor_copy(RA[r][0:D, 0:3 * D], psB[0][0:D, r * 3 * D:(r + 1) * 3 * D])
                ins = V.tensor_copy(RB[r][0:D + AW, 0:3 * D], psB[1][0:D + AW, r * 3 * D:(r + 1) * 3 * D])
            ins.then_inc(ones_set, 1)

            def stage_src(q, i, n):
                if not (peeled(i) and i == 0 and n == 0):
                    dve.wait_ge(gathered[q], n * (16 * GC))
                V.tensor_copy(src_st[q][:, :], src_c[:, bass.ds((i * 2 + q) * GC, GC)]).then_inc(src_staged[q], 1)

            def edge_pass(p):
                def body(i):
                    for q in range(2):
                        n = edge_base(p) + i
                        c0 = (i * 2 + q) * GC
                        if p != "aux":
                            stage_src(q, i, gather_base(p) + i)
                        begin_all = p == "aux" and peeled(i) and i == 0
                        if not begin_all:
                            dve.wait_ge(combined[q], n)
                        for c in range(GC):
                            if p == "aux" or p in GRU:
                                ins = V.tensor_scalar(sel[q][:, c, :], lane[:, :], first_c[:, bass.ds(c0 + c, 1)],
                                                      None, ALU.is_equal)
                            else:
                                ins = V.tensor_scalar(sel[q][:, c, :], lane[:, :], first_c[:, bass.ds(c0 + c, 1)],
                                                      edge_w[:, bass.ds(c0 + c, 1)], ALU.is_equal, ALU.mult)
                        ins.then_inc(sel_built[q], 1)
                        if not begin_all:
                            dve.wait_ge(scattered[q], n * (16 * GC))
                        V.tensor_copy(dst_st[q][:, :], dst_idx[:, bass.ds(c0, GC)]).then_inc(dst_staged[q], 1)
                walk(dve, HALF, body)
                old, new, w = (cold_aux, cnew_aux, AW) if p == "aux" else (cold, cnew, D)
                dve.wait_ge(c_combined, carry_no(p) + 1)
                dve.wait_ge(c_gathered, 16 * C_ROWS * (carry_no(p) + 1))
                V.tensor_tensor(new[:, :, :], old[:, :, :], psB[0][:, 0:CB * w].rearrange("p (b d) -> p b d", d=w),
                                ALU.add).then_inc(c_added, 1)

            edge_pass("aux")
            for k in range(8):
                dve.wait_ge(aux_loaded, 16 * (k + 1))
                V.tensor_scalar(deg[:, k * WB:(k + 1) * WB],
                                wide[:, 0:WB * AW].rearrange("p (k d) -> p k d", d=AW)[:, :, DE],
                                1.0, None, ALU.add).then_inc(s_done, 1)
            dve.wait_ge(deg_root, 1)
            V.reciprocal(s_big[:, :], deg[:, :]).then_inc(s_ready, 1)

            def w_copy(q, i):
                n = gather_base("w") + i
                dve.wait_ge(gathered[q], (n + 1) * (16 * GC))
                V.tensor_copy(edge_w[:, bass.ds((i * 2 + q) * GC, GC)], w_st[q][:, :]).then_inc(w_copied[q], 1)

            def w_body(i):
                for q in range(2):
                    if not (peeled(i) and i == 0):
                        w_copy(q, i - 1)
                    stage_src(q, i, gather_base("w") + i)
            walk(dve, HALF, w_body)
            for q in range(2):
                w_copy(q, HALF - 1)
                dve.wait_ge(w_copied[q], HALF)

            def centre(l, a):
                n, z, st = ln_base(l) + a.no, z_t[a.q], st_t[a.q]
                dve.wait_ge(z_ready, n + 1)
                V.tensor_reduce(st[:, 0, :], z[:, :, :], AX.X, ALU.add).then_inc(n_sum, 1)
                dve.wait_ge(n_sum, n + 1)
                V.scalar_tensor_tensor(xc_t[a.q][:, :, :], st[:, 0, :].rearrange("p (j a) -> p j a", a=1)
                                       .to_broadcast([P, NPP, D]), -1.0 / D, z[:, :, :], ALU.mult, ALU.add
                                       ).then_inc(n_centred, 1)

            def variance(l, a):
                n = ln_base(l) + a.no
                dve.wait_ge(n_squared, n + 1)
                V.tensor_reduce(st_t[a.q][:, 2, :], sq_t[a.q][:, :, :], AX.X, ALU.add).then_inc(n_var, 1)

            def inverse_root(l, a):
                st, k = st_t[a.q], [0]
                v, y, u = st[:, 3, :], st[:, 1, :], st[:, 4, :]

                def link(ins):
                    k[0] += 1
                    ins.then_inc(newton, 1)
                    dve.wait_ge(newton, a.no * NEWTON + k[0])

                dve.wait_ge(n_var, ln_base(l) + a.no + 1)
                link(V.tensor_scalar(v, st[:, 2, :], 1.0 / D, EPS, ALU.mult, ALU.add))
                link(V.tensor_scalar(u.bitcast(i32), v.bitcast(i32), 1, None, ALU.arith_shift_right))
                link(V.tensor_scalar(y.bitcast(i32), u.bitcast(i32), -1.0, float(0x5f3759df), ALU.mult, ALU.add))
                for _ in range(3):
                    link(V.tensor_tensor(u, y, y, ALU.mult))
                    link(V.scalar_tensor_tensor(st[:, 5, :], u, -0.5, v, ALU.mult, ALU.mult))
                    link(V.scalar_tensor_tensor(y, st[:, 5, :], 1.5, y, ALU.add, ALU.mult))

            def normalise(l, a):
                n, st = ln_base(l) + a.no, st_t[a.q]
                if l not in GRU:
                    dve.wait_ge(n_std, n_std_base(l) + a.no + 1)
                    V.reciprocal(st[:, 1, :], st[:, 3, :]).then_inc(n_rstd, 1)
                    dve.wait_ge(n_rstd, n_std_base(l) + a.no + 1)
                if not a.early:
                    dve.wait_ge(stored[a.q], 16 * BT * l + a.pair * 16)
                V.tensor_tensor(o_t[a.q][:, :, :], xc_t[a.q][:, :, :], st[:, 1, :].rearrange("p (j a) -> p j a", a=1)
                                .to_broadcast([P, NPP, D]), ALU.mult).then_inc(finished, 1)

            for l in range(LAYERS):
                edge_pass(l)
                if l in GRU:
                    def body(i):
                        for k in range(2 * SLOTS):
                            u = unit_at(i, k, 0)
                            if u.there:
                                dve.wait_ge(g_transposed, gru_base(l) + u.no + 1)
                                if not u.early:
                                    dve.wait_ge(g_mm, gru_base(l) + u.no - 1)
                                V.tensor_copy(bT[u.g][:, :], psB[u.g][0:KB, :]).then_inc(bT_ready, 1)
                            u = unit_at(i, k, 1)
                            if u.there:
                                n = gru_base(l) + u.no
                                dve.wait_ge(gates, n + 1)
                                V.tensor_tensor(d3_t[u.g][:, :, :], rz_t[u.g][:, :, 0:D], psG[u.g][:, :, 3 * D:GW],
                                                ALU.mult).then_inc(n_prod, 1)
                                if not u.early:
                                    dve.wait_ge(n_act, n - 1)
                                dve.wait_ge(n_prod, n + 1)
                                V.tensor_tensor(d2_t[u.g][:, :, :], d3_t[u.g][:, :, :], psG[u.g][:, :, 2 * D:3 * D],
                                                ALU.add).then_inc(n_pre, 1)
                            if l in LN and k % 2 == 0:
                                b = tile_at(i, k // 2, 3)
                                if b.there:
                                    variance(l, b)
                                    inverse_root(l, b)
                            if l in LN and k % 2 == 1:
                                a, c = (tile_at(i, k // 2, lag) for lag in (2, 3))
                                if a.there:
                                    dve.wait_ge(g_new, gru_base(l) + a.no * 2 + 2)
                                    dve.wait_ge(loaded[a.r], load_base(l, a.r) + (a.step + 1) * (16 * LOADS[l]))
                                    V.tensor_tensor(z_t[a.q][:, :, :], z_t[a.q][:, :, :], res_t[a.r][:, :, :],
                                                    ALU.add).then_inc(z_ready, 1)
                                if c.there:
                                    normalise(l, c)
                                if a.there:
                                    centre(l, a)
                    pipeline(dve, body, 3)
                else:
                    w = {0: 0, 1: 1, 2: 2, 5: 3}[l]
                    bias_b = bias[w][:, :].rearrange("p (a d) -> p a d", a=1).to_broadcast([P, NPP, D])

                    def body(i):
                        for k in range(SLOTS):
                            a, b, c = (tile_at(i, k, lag) for lag in (0, 1, 2))
                            q = a.q
                            z = z_t[q]
                            if a.there:
                                n = gcn_base(l) + a.no
                                dve.wait_ge(mm_done, n + 1)
                                if l == 0 and not a.early:
                                    dve.wait_ge(finished, a.no - 1)
                                zb = z if l == 0 else za_t[q]
                                V.tensor_tensor(zb[:, :, :], psB[q][:, :].rearrange("p (j d) -> p j d", d=D), bias_b,
                                                ALU.add).then_inc(z_biased, 1)
                                if l == 0:
                                    continue
                                m = ln_base(l) + a.no
                                dve.wait_ge(z_biased, n + 1)
                                if l == 1:
                                    dve.wait_ge(loaded[a.r], load_base(l, a.r) + (a.step + 1) * (16 * LOADS[l]))
                                    V.tensor_tensor(z[:, :, :], zb[:, :, :], res_t[a.r][:, :, :], ALU.add
                                                    ).then_inc(z_ready, 1)
                                elif l == 2:
                                    V.scalar_tensor_tensor(z[:, :, :], zb[:, :, :], 0.1, zb[:, :, :], ALU.mult,
                                                           ALU.max).then_inc(z_acted, 1)
                                    dve.wait_ge(z_acted, a.no + 1)
                                    V.tensor_tensor(z[:, :, :], z[:, :, :], h_t[a.r][:, :, :], ALU.add
                                                    ).then_inc(z_ready, 1)
                                else:
                                    V.scalar_tensor_tensor(z[:, :, :], zb[:, :, :], 0.0, h_t[a.r][:, :, :], ALU.max,
                                                           ALU.add).then_inc(z_ready, 1)
                            if l and c.there:
                                normalise(l, c)
                            if a.there:
                                centre(l, a)
                            if l and b.there:
                                variance(l, b)
                    pipeline(dve, body, 2)

        @block.tensor
        def _(pe):
            pe.wait_ge(prep_t, 1)
            for b in range(CB):
                a = 1
                nc.tensor.transpose(psA[0][:, b * P:(b + 1) * P], first[a][:, b, :], ident[:, :])
                ins = nc.tensor.transpose(psA[1][:, b * P:(b + 1) * P], first[1 - a][:, b, :], ident[:, :])
            ins.then_inc(fold_mm, 1)
            for r in range(2):
                c = slice(r * 3 * D, (r + 1) * 3 * D)
                nc.tensor.matmul(psB[0][0:D, c], wms[r][:, :], wih[r][:, :], start=True, stop=True)
                ins = nc.tensor.matmul(psB[1][0:D + AW, c], wmd[r][:, :], wih[r][:, :], start=True, stop=True)
            ins.then_inc(fold_mm, 1)
            pe.wait_ge(ones_set, 1)
            pe.wait_ge(bias_rows, 32)
            pe.wait_ge(bw_loaded, 16 * 12)

            def edge_pass(p):
                src, w = (erows, AW) if p == "aux" else (rows, D)

                def body(i):
                    for q in range(2):
                        n = edge_base(p) + i
                        if p == "aux":
                            pe.wait_ge(e_loaded[q], (i + 1) * 16)
                        else:
                            pe.wait_ge(gathered[q], (gather_base(p) + i + 1) * (16 * GC))
                        pe.wait_ge(sel_built[q], n + 1)
                        if not (p == "aux" and peeled(i) and i == 0):
                            pe.wait_ge(sums_out[q], n)
                        ps = psG[q][:, :, :].rearrange("p a b -> p (a b)")
                        for c in range(GC):
                            ins = nc.tensor.matmul(ps[:, c * w:(c + 1) * w], sel[q][:, c, :], src[q][:, c, :],
                                                   start=True, stop=True)
                        ins.then_inc(combined[q], 1)
                walk(pe, HALF, body)
                pe.wait_ge(c_loaded, 32 * (carry_no(p) + 1))
                cb = cbuf_aux if p == "aux" else cbuf
                for b in range(CB):
                    for k in range(CB):
                        ins = nc.tensor.matmul(psB[0][:, b * w:(b + 1) * w], same[:, k, b * P:(b + 1) * P],
                                               cb[:, k, :], start=(k == 0), stop=(k == CB - 1))
                ins.then_inc(c_combined, 1)

            edge_pass("aux")
            for l in range(LAYERS):
                edge_pass(l)
                if l in GRU:
                    r = GRU.index(l)

                    def body(i):
                        for k in range(2 * SLOTS):
                            u = unit_at(i, k, 0)
                            if u.there:
                                q, r4, g, n = u.tile.q, u.tile.r, u.g, gru_base(l) + u.no
                                if g == 0:
                                    pe.wait_ge(loaded[r4], load_base(l, r4) + (u.tile.step + 1) * (16 * LOADS[l]))
                                    pe.wait_ge(b_ready, gru_base(l) + u.no + 2)
                                if not u.early:
                                    pe.wait_ge(aT_ready, n - 1)
                                    pe.wait_ge(bT_ready, n - 1)
                                for j in range(HN):
                                    nc.tensor.transpose(psA[g][:, j * P:(j + 1) * P], ah_t[r4][:, g * HN + j, :],
                                                        ident[:, :])
                                    ins = nc.tensor.transpose(psB[g][0:KB, j * P:(j + 1) * P],
                                                              b_t[q][:, g * HN + j, :], ident[:, :])
                                ins.then_inc(g_transposed, 1)
                            u = unit_at(i, k, 1)
                            if u.there:
                                g, n = u.g, gru_base(l) + u.no
                                pe.wait_ge(aT_ready, n + 1)
                                pe.wait_ge(bT_ready, n + 1)
                                if not u.early:
                                    pe.wait_ge(n_pre, n - 1)
                                for j in range(HN):
                                    nc.tensor.matmul(psG[g][:, j, :], aT[g][:, j * P:(j + 1) * P], RA[r][:, :],
                                                     start=True, stop=False)
                                    ins = nc.tensor.matmul(psG[g][:, j, :], bT[g][:, j * P:(j + 1) * P],
                                                           RB[r][:, :], start=False, stop=True)
                                ins.then_inc(g_mm, 1)
                    pipeline(pe, body, 1)
                else:
                    w = {0: 0, 1: 1, 2: 2, 5: 3}[l]

                    def body(i):
                        for k in range(SLOTS):
                            a, b = tile_at(i, k, 0), tile_at(i, k, 1)
                            if a.there:
                                n, q = gcn_base(l) + a.no, a.q
                                pe.wait_ge(y_ready, n + 1)
                                if not a.early:
                                    pe.wait_ge(yT_ready, n - 1)
                                for j in range(NPP // 2):
                                    ins = nc.tensor.transpose(psA[q][:, j * P:(j + 1) * P],
                                                              y_t[q][:, 2 * j:2 * j + 2, :]
                                                              .rearrange("p a d -> p (a d)"), ident[:, :])
                                ins.then_inc(y_transposed, 1)
                            if b.there:
                                n = gcn_base(l) + b.no
                                pe.wait_ge(yT_ready, n + 1)
                                if not b.early:
                                    pe.wait_ge(z_biased, n - 1)
                                for j in range(NPP // 2):
                                    ins = nc.tensor.matmul(psB[b.q][:, j * P:(j + 1) * P],
                                                           yT[b.q][:, j * P:(j + 1) * P], BW[w][:, :],
                                                           start=True, stop=True)
                                ins.then_inc(mm_done, 1)
                    pipeline(pe, body, 1)


def kernel(**inputs):
    import numpy as np
    import concourse.bacc as bacc
    from concourse.bass_utils import run_bass_kernel_spmd as run

    g = {k: np.asarray(v) for k, v in inputs.items()}
    pad = CB * P * P
    src = np.concatenate([g["src"], np.zeros(CHUNKS * P - E, np.int32)])
    dst = np.concatenate([g["dst"], np.full(pad - E, N, np.int32)])
    before = np.concatenate([np.full(P + 1, -1, np.int32), dst])

    def by_chunk(a):
        return a.reshape(CB, P, P).transpose(1, 0, 2).reshape(P, CB * P)

    arrays = {
        "x": g["x"],
        "edges": np.concatenate([g["edge_attr_16"], np.zeros((CHUNKS * P - E, DE), np.float32)]),
        "src_cols": src.reshape(CHUNKS, P).T,
        "dst_rows": by_chunk(dst),
        "prev_rows": by_chunk(before[P:P + pad]),
        "back": before[0:pad:P].reshape(CB, P).T,
        "head": np.broadcast_to(dst[0:pad:P], (P, CB * P)),
    }
    for l, (w, b) in enumerate([(g["L0_gnn_W1"].T, "L0_gnn_b1"), (g["L0_gnn_W2"].T, "L0_gnn_b2"),
                                (g["L1_gnn_weight"], "L1_gnn_bias"), (g["L3_gnn_W"].T, "L3_gnn_b")]):
        arrays[f"w{l}"] = w
        arrays[f"bias{l}"] = np.broadcast_to(g[b], (P, D))
    zero = np.zeros(D, np.float32)
    for r in range(2):
        wm, bm = g["L2_gnn_W_msg"][r], g["L2_gnn_b_msg"][r]
        arrays[f"wms{r}"] = wm[D:2 * D].T
        arrays[f"wmd{r}"] = np.concatenate([wm[0:D], wm[2 * D:], bm[None]]).T
        arrays[f"wih{r}"] = g["L2_gnn_W_ih"][r].T
        arrays[f"whh{r}"] = g["L2_gnn_W_hh"][r].T
        bi, bh = g["L2_gnn_b_ih"][r], g["L2_gnn_b_hh"][r]
        arrays[f"gbias{r}"] = np.stack([np.concatenate([bi, zero]), np.concatenate([bh[:2 * D], zero, bh[2 * D:]])])

    nc = bacc.Bacc("TRN2", target_bir_lowering=False, num_devices=1)
    feed, aps = {}, {}
    for name, a in arrays.items():
        feed[f"{name}_dram"] = np.ascontiguousarray(a)
        aps[name] = nc.dram_tensor(f"{name}_dram", a.shape, mybir.dt.from_np(a.dtype), kind="ExternalInput").ap()
    aps["out"] = nc.dram_tensor("out_dram", (N, D), mybir.dt.float32, kind="ExternalOutput").ap()
    build(nc, aps)
    r = run(nc, [feed], core_ids=[0])
    return r.results[0]["out_dram"]
```

```python
import concourse.bass as bass
from concourse import mybir
from contextlib import ExitStack

N = 100000
E = 50000
D = 64
DE = 16
P = 128
NPP = 8
TILE = P * NPP
TILES = -(-N // TILE)
NPAD = TILES * TILE
LASTP = (N - (TILES - 1) * TILE) // NPP
GP = 2
GC = 2 * GP
EP = 2 * P
SL = 3
STEPS = -(-E // (P * GC * SL))
GROUPS = SL * STEPS
CHUNKS = GROUPS * GC
PAIRS = GROUPS * GP
CB = -(-PAIRS // P)
LASTC = PAIRS - (CB - 1) * P
QN = 5
AW = DE + 1
EW = AW + 1
KB = D + AW + 2
GW = 4 * D
ROUND = 1.5 * (1 << 23)
FAR = float(1 << 20)
EPS = 1e-5
LAYERS = 6
GRU = (3, 4)
SCALED = (0, 1)
WITH_S = (2, 5)
DS = D + 1
LN = (1, 2, 4, 5)
LOADS = (3, 4, 2, 3, 3, 2)
LAG = (0, 2, 2, 0, 3, 2)
SLOTS = 4
NEWTON = 12
UNITS = 2 * TILES
HN = NPP // 2


def build(nc, t):
    f32, i32 = mybir.dt.float32, mybir.dt.int32
    ALU, ACT, AX = mybir.AluOpType, mybir.ActivationFunctionType, mybir.AxisListType
    with ExitStack() as ctx:
        def sb(name, shape, dt=f32):
            return ctx.enter_context(nc.sbuf_tensor(name, shape, dt))

        def two(name, shape, dt=f32):
            return [sb(f"{name}{q}", shape, dt) for q in range(2)]

        def three(name, shape, dt=f32):
            return [sb(f"{name}{q}", shape, dt) for q in range(SL)]

        def sem(name):
            return ctx.enter_context(nc.semaphore(name))

        def sems(name):
            return [sem(f"{name}{q}") for q in range(2)]

        def slot_sems(name):
            return [[sem(f"{name}{m}_{q}") for q in range(SL)] for m in range(2)]

        def dram(name, shape):
            return nc.dram_tensor(name, shape, f32).ap()

        agg = dram("agg", (NPAD, D))
        aux = dram("aux", (NPAD, AW))
        carry = dram("carry", (PAIRS, QN * D))
        carry_aux = dram("carry_aux", (PAIRS, QN * AW))
        s_tab = dram("s_tab", (NPAD, 1))
        xs, h1s, x2, v1 = (dram(n, (NPAD, D)) for n in ("xs", "h1s", "x2", "v1"))
        x1, x3 = (dram(n, (NPAD, DS)) for n in ("x1", "x3"))
        layer_in = [xs, h1s, x1, x2, v1, x3]
        layer_res = [None, t["x"], None, None, x2, None]
        layer_out = [h1s, x1, x2, v1, x3, t["out"]]

        WB = NPAD // P // 8
        zeros = sb("zeros", [P, WB * AW])
        ZR = -(-NPAD // P // STEPS)
        wide = sb("wide", [P, WB * D])

        def shaped(bufs, pattern, **sizes):
            return [b[:, :].rearrange(pattern, **sizes) for b in bufs]

        by_node = "p (j d) -> p j d"
        in_t = [sb(f"in_t{r}", [P, NPP * (DS + D)]) for r in range(SLOTS)]
        h_t = [b[:, 0:NPP * D].rearrange(by_node, d=D) for b in in_t]
        hs_t = [b[:, 0:NPP * DS].rearrange(by_node, d=DS) for b in in_t]
        agg_t = [b[:, NPP * DS:].rearrange(by_node, d=D) for b in in_t]
        ah_t = [b[:, 0:NPP * 2 * D].rearrange(by_node, d=2 * D) for b in in_t]
        res_t = [sb(f"res_t{r}", [P, NPP, D]) for r in range(SLOTS)]
        s_t = [sb(f"s_t{r}", [P, NPP]) for r in range(SLOTS)]
        s_keep = [sb(f"s_keep{r}", [P, NPP]) for r in range(SLOTS)]
        aux_t = [sb(f"aux_t{r}", [P, NPP, AW]) for r in range(SLOTS)]
        work = {n: two(n, [P, NPP * D]) for n in ("y", "y0", "y1", "yT", "z", "za", "xc", "sq")}
        out_w = two("out_w", [P, NPP * DS])
        o_t = [b[:, 0:NPP * D].rearrange(by_node, d=D) for b in out_w]
        os_t = shaped(out_w, by_node, d=DS)
        y_t, y0_t, y1_t, z_t, za_t, xc_t, sq_t = (shaped(work[n], by_node, d=D) for n in
                                                       ("y", "y0", "y1", "z", "za", "xc", "sq"))
        z2_t = [b.rearrange(by_node, d=D) for b in (wide[:, 0:NPP * D], wide[:, NPP * D:2 * NPP * D])]
        yT = work["yT"]
        aT = work["yT"]
        bT = [b[0:KB, :] for b in work["za"]]
        rz_t = shaped(work["y"], by_node, d=2 * D)
        d2_t, d3_t = ([b[:, k * HN * D:(k + 1) * HN * D].rearrange(by_node, d=D) for b in work["y0"]] for k in range(2))
        m_t, d_t = ([b[:, k * HN * D:(k + 1) * HN * D].rearrange(by_node, d=D) for b in work["y1"]] for k in range(2))
        n_t = two("n_t", [P, HN, D])
        st_t = two("st_t", [P, 6, NPP])
        b_t = two("b_t", [P, NPP, KB])

        by_half = "p (b e) -> p b e"
        blk, node, prv_block, begin, block_mark = (work[n][0][:, :].rearrange(by_half, b=CB)
                                               for n in ("y", "y0", "y1", "yT", "z"))
        rank = shaped(work["xc"], by_half, b=CB)
        high = work["za"][0][:, 0:CB]
        any_high = work["za"][1][0:1, 0:1]
        dst_r, prv_r = (b[:, 0:CB * EP].bitcast(i32) for b in out_w)
        dst_f = work["y"][1][:, :]
        cols_i = sb("cols_i", [P, P], i32)
        cols = sb("cols", [P, P])
        part_i = sb("part_i", [P, 1], i32)
        part = sb("part", [P, 1])
        ident = sb("ident", [P, P])
        src_c = sb("src_c", [P, CHUNKS], i32)
        back_r = sb("back_r", [P, CB], i32)
        head_r = sb("head_r", [P, CB * P], i32)
        back_block = sb("back_block", [P, CB])
        head_block = sb("head_block", [P, CB * P])
        rank_c = two("rank_c", [P, CHUNKS])
        node_c = sb("node_c", [P, CHUNKS, QN])
        mark_c = sb("mark_c", [P, CHUNKS, 1])
        more = sb("more", [1, 1], i32)
        dst_idx = two("dst_idx", [P, PAIRS], i32)
        cont = sb("cont", [P, CB])
        lead = sb("lead", [P, CB])
        cidx_f = sb("cidx_f", [P, CB])
        carry_src = sb("carry_src", [P, CB], i32)
        carry_dst = sb("carry_dst", [P, CB], i32)
        same = sb("same", [P, CB, CB * P])
        deg = sb("deg", [P, NPAD // P])
        eps = sb("eps", [P, 1])
        s_big = sb("s_big", [P, NPAD // P])
        BW = [sb(f"bw{l}", [P, P]) for l in range(4)]
        bf16 = mybir.dt.bfloat16
        bias = sb("bias", [P, 4, D])
        bias_left = two("bias_left", [P, 4, D])
        bias_part = [sb(f"bias_part{k}", [P, 4, D], bf16) for k in range(3)]
        bias_rows3 = [sb(f"bias_rows3_{l}", [P, NPP, D], bf16) for l in range(4)]
        ones3 = sb("ones3", [3, P], bf16)
        wms = [sb(f"wms{r}", [P, D]) for r in range(2)]
        wmd = [sb(f"wmd{r}", [P, D + AW]) for r in range(2)]
        wih = [sb(f"wih{r}", [P, 3 * D]) for r in range(2)]
        RA = [sb(f"ra{r}", [P, GW]) for r in range(2)]
        RB = [sb(f"rb{r}", [KB, GW]) for r in range(2)]

        src_st = three("src_st", [P, GC], i32)
        dst_st = three("dst_st", [P, GP], i32)
        rows = three("rows", [P, GC, DS])
        erows = three("erows", [P, GC, AW])
        piece = [wide[:, k * WB * AW:(k + 1) * WB * AW] for k in range(3)]
        SELW, SPRW = GC * P, GC * QN * D
        sel = [wide[:, q * SELW:(q + 1) * SELW].rearrange("p (c n) -> p c n", n=P) for q in range(SL)]
        spread = [wide[:, SL * SELW + q * SPRW:SL * SELW + (q + 1) * SPRW] for q in range(SL)]
        srows = [b.rearrange("p (c a d) -> p c a d", c=GC, a=QN) for b in spread]
        esrows = [b[:, 0:GC * QN * EW].rearrange("p (c a d) -> p c a d", c=GC, a=QN) for b in spread]
        sums = three("sums", [P, GP, QN * D])
        esums = three("esums", [P, GP, QN, AW])
        marks = three("marks", [P, GP])
        cbuf = sb("cbuf", [P, CB, QN * D])
        cbuf_aux = sb("cbuf_aux", [P, CB, QN * AW])
        cold = sb("cold", [P, CB, QN * D])
        cold_aux = sb("cold_aux", [P, CB, QN * AW])
        cnew = sb("cnew", [P, CB, QN * D])
        cnew_aux = sb("cnew_aux", [P, CB, QN * AW])

        psA = [ctx.enter_context(nc.psum_tensor(f"psA{q}", [P, 512], f32)) for q in range(2)]
        psB = [ctx.enter_context(nc.psum_tensor(f"psB{q}", [P, 512], f32)) for q in range(2)]
        psG = [ctx.enter_context(nc.psum_tensor(f"psG{q}", [P, HN, GW], f32)) for q in range(2)]
        banks = [g[:, :, :].rearrange("p a b -> p (a b)")[:, h * 512:(h + 1) * 512] for g in psG for h in range(2)]
        banks += [b[:, :] for b in psA]
        psS = [banks[q * GP:(q + 1) * GP] for q in range(SL)]

        in_loaded = sem("in_loaded")
        bw_zeroed = sem("bw_zeroed")
        bw_loaded = sem("bw_loaded")
        zeros_set = sem("zeros_set")
        aux_zeroed, agg_zeroed = sem("aux_zeroed"), sem("agg_zeroed")
        iotas = sem("iotas")
        prep = sem("prep")
        prep_t = sem("prep_t")
        prep_w = sem("prep_w")
        fold_mm = sem("fold_mm")
        ones_set = sem("ones_set")
        bias_rows = sem("bias_rows")
        aux_loaded = [sem(f"aux_loaded{k}") for k in range(3)]
        s_done = sem("s_done")
        deg_root = sem("deg_root")
        s_ready = sem("s_ready")
        eps_set = sem("eps_set")
        s_stored = sem("s_stored")
        src_staged, dst_staged = slot_sems("src_staged"), slot_sems("dst_staged")
        gathered, e_loaded = slot_sems("gathered"), slot_sems("e_loaded")
        spread_out, combined, sums_out = slot_sems("spread_out"), slot_sems("combined"), slot_sems("sums_out")
        scattered = slot_sems("scattered")
        marks_out, idx_set = slot_sems("marks_out"), slot_sems("idx_set")
        carried = [sem(f"carried{q}") for q in range(SL)]
        pool_turn = sem("pool_turn")
        c_loaded, c_combined, c_gathered = sem("c_loaded"), sem("c_combined"), sem("c_gathered")
        c_added, c_scattered = sem("c_added"), sem("c_scattered")
        x_loaded, x_stored = ([sem(f"{n}{r}") for r in range(SLOTS)] for n in ("x_loaded", "x_stored"))
        x_scaled = sem("x_scaled")
        loaded, stored = [sem(f"loaded{r}") for r in range(SLOTS)], sems("stored")
        newton = sem("newton")
        res_loaded = [sem(f"res_loaded{r}") for r in range(SLOTS)]
        finished = sem("finished")
        y_scaled, y_summed, y_ready = sem("y_scaled"), sem("y_summed"), sem("y_ready")
        y_transposed, yT_ready, mm_done = sem("y_transposed"), sem("yT_ready"), sem("mm_done")
        z_copied, z_acted, z_ready = sem("z_copied"), sem("z_acted"), sem("z_ready")
        n_sum, n_mean, n_centred = sem("n_sum"), sem("n_mean"), sem("n_centred")
        n_squared, n_var, n_std, n_rstd = sem("n_squared"), sem("n_var"), sem("n_std"), sem("n_rstd")
        b_ready, g_transposed = sem("b_ready"), sem("g_transposed")
        ops_ready, g_mm = sem("ops_ready"), sem("g_mm")
        gates, n_prod, n_pre, n_act = sem("gates"), sem("n_prod"), sem("n_pre"), sem("n_act")
        g_diff, g_scaled, g_new = sem("g_diff"), sem("g_scaled"), sem("g_new")

        def edge_base(p):
            return 0 if p == "aux" else STEPS * (1 + p)

        def gather_base(p):
            return STEPS * p

        def carry_no(p):
            return 0 if p == "aux" else 1 + p

        def gcn_base(l):
            return TILES * sum(k not in GRU for k in range(l))

        def ln_base(l):
            return TILES * sum(k in LN for k in range(l))

        def n_std_base(l):
            return TILES * sum(k in LN and k not in GRU for k in range(l))

        def gru_base(l):
            return UNITS * sum(k in GRU for k in range(l))

        def load_base(l, r):
            return 16 * (-(-(TILES - r) // SLOTS)) * sum(LOADS[:l])

        def walk(eng, n, body):
            body(0)
            with eng.Fori(1, n - 1) as i:
                body(i)
            body(n - 1)

        def peeled(i):
            return isinstance(i, int)

        def both_parts(eng, has_more, p, part):
            part(p, 0)
            with eng.If(has_more > 0):
                for q in range(SL):
                    eng.wait_ge(scattered[0][q], 16 * GP * (edge_base(p) + STEPS))
                    eng.wait_ge(carried[q], 16 * (edge_base(p) + STEPS))
                part(p, 1)
                for q in range(SL):
                    eng.wait_ge(scattered[1][q], 16 * GP * (edge_base(p) + STEPS))

        class Tile:
            def __init__(self, step, k):
                self.no = step * SLOTS + k
                self.step, self.r, self.q = step, k, k % 2
                self.pair = step * 2 + k // 2
                self.there = not peeled(step) or 0 <= self.no < TILES
                self.early = peeled(step) and self.no < 2

        class Unit:
            def __init__(self, step, k):
                self.tile = Tile(step, k // 2)
                self.g = k % 2
                self.no = step * (2 * SLOTS) + k
                self.there = self.tile.there
                self.early = peeled(step) and self.no < 2

        def tile_at(i, k, lag):
            return Tile(i + (k - lag) // SLOTS, (k - lag) % SLOTS)

        def unit_at(i, k, lag):
            return Unit(i + (k - lag) // (2 * SLOTS), (k - lag) % (2 * SLOTS))

        def pipeline(eng, body, lag, stop=TILES // SLOTS):
            lead = -(-lag // SLOTS)
            for i in range(lead):
                body(i)
            with eng.Fori(lead, stop) as i:
                body(i)
            for i in range(stop, -(-(TILES + lag) // SLOTS)):
                body(i)

        BT = TILES // 2
        in_names = ("src_cols", "dst_rows", "prev_rows", "back", "head")
        PREP_LOADS = len(in_names) + 4 + 2 * 3
        C_ROWS = CB

        block = ctx.enter_context(nc.Block())

        @block.sync
        def _(sp):
            for name, buf in zip(in_names, (src_c, dst_r, prv_r, back_r, head_r)):
                sp.dma_start(buf[:, :], t[name]).then_inc(in_loaded, 16)
            for l in range(4):
                sp.dma_start(bias[:, l, :], t[f"bias{l}"]).then_inc(in_loaded, 16)
            for r in range(2):
                sp.dma_start(wms[r][:, :], t[f"wms{r}"]).then_inc(in_loaded, 16)
                sp.dma_start(wmd[r][:, :], t[f"wmd{r}"]).then_inc(in_loaded, 16)
                sp.dma_start(wih[r][:, :], t[f"wih{r}"]).then_inc(in_loaded, 16)
            sp.wait_ge(bw_zeroed, 1)
            for l in range(4):
                sp.dma_start(BW[l][0:D, 0:D], t[f"w{l}"]).then_inc(bw_loaded, 16)
                sp.dma_start(BW[l][D:P, D:P], t[f"w{l}"]).then_inc(bw_loaded, 16)
            for r in range(2):
                sp.dma_start(RA[r][D:P, 0:2 * D], t[f"whh{r}"][:, 0:2 * D]).then_inc(bw_loaded, 16)
                sp.dma_start(RA[r][D:P, 3 * D:GW], t[f"whh{r}"][:, 2 * D:3 * D]).then_inc(bw_loaded, 16)
            sp.wait_ge(zeros_set, 1)
            for k in range(8):
                sp.dma_start(aux.rearrange("(p k) d -> p (k d)", p=P)[:, k * WB * AW:(k + 1) * WB * AW],
                             zeros[:, 0:WB * AW]).then_inc(aux_zeroed, 16)
            sp.wait_ge(ones_set, 1)
            for r in range(2):
                sp.dma_start(RB[r][KB - 2:KB, :], t[f"gbias{r}"]).then_inc(bias_rows, 16)

            sp.wait_ge(prep, 1)
            has_more = sp.value_load(more[0:1, 0:1], min_val=0, max_val=1)

            def part(p, m):
                out, table = (esums, carry_aux) if p == "aux" else (sums, carry)

                def load_features(q, i):
                    sp.dma_start(erows[q][:, :, 0:DE], t["edges"][bass.ds((i * SL + q) * (GC * P), GC * P), :]
                                 .rearrange("(c p) d -> p c d", p=P)).then_inc(e_loaded[m][q], 16)

                if p == "aux":
                    for q in range(SL):
                        load_features(q, 0)

                def body(i):
                    if p == "aux" and not (peeled(i) and i == STEPS - 1):
                        for q in range(SL):
                            sp.wait_ge(spread_out[m][q], i + 1)
                            load_features(q, i + 1)
                    for q in range(SL):
                        n = edge_base(p) + i
                        if m == 0:
                            sp.wait_ge(sums_out[m][q], n + 1)
                            src = out[q][0:1, :, :]
                            if p == "aux":
                                src = out[q][0:1, :, :, :].rearrange("p c a d -> p c (a d)")
                            sp.dma_start(table[bass.ds((i * SL + q) * GP, GP), :].rearrange("(a c) d -> a c d", a=1),
                                         src).then_inc(carried[q], 16)
                if m == 0 or p == "aux":
                    walk(sp, STEPS, body)

            def edge_pass(p):
                both_parts(sp, has_more, p, part)
                table = carry_aux if p == "aux" else carry
                for q in range(SL):
                    sp.wait_ge(carried[q], 16 * (edge_base(p) + STEPS))
                dst = cbuf_aux if p == "aux" else cbuf
                full = (CB - 1) * P
                sp.dma_start(dst[:, 0:CB - 1, :], table[0:full, :].rearrange("(b p) d -> p b d", p=P)
                             ).then_inc(c_loaded, 16)
                sp.dma_start(dst[0:LASTC, CB - 1, :], table[full:PAIRS, :]).then_inc(c_loaded, 16)

            edge_pass("aux")
            sp.wait_ge(c_scattered, 16 * C_ROWS)
            av = aux.rearrange("(p k) d -> p (k d)", p=P)
            for k in range(8):
                if k >= 3:
                    sp.wait_ge(s_done, k - 2)
                sp.dma_start(piece[k % 3], av[:, k * WB * AW:(k + 1) * WB * AW]).then_inc(aux_loaded[k % 3], 16)
            sp.wait_ge(s_ready, 1)
            sp.dma_start(s_tab.rearrange("(p k) a -> p (k a)", p=P), s_big[:, :]).then_inc(s_stored, 16)

            def view(tab, tile, parts=P):
                return tab[bass.ds(tile * TILE, parts * NPP), :].rearrange("(p j) d -> p j d", p=parts)

            def load_s(tile, r, done):
                sp.dma_start(s_t[r][:, :], s_tab[bass.ds(tile * TILE, TILE), :]
                             .rearrange("(p j) a -> p (j a)", p=P)).then_inc(done, 16)

            sp.wait_ge(s_stored, 16)

            def load_x(tile, r):
                parts = LASTP if peeled(tile) and tile == TILES - 1 else P
                sp.dma_start(h_t[r][0:parts, :, :], view(t["x"], tile, parts)).then_inc(x_loaded[r], 16)
                load_s(tile, r, x_loaded[r])

            for r in range(SLOTS):
                load_x(r, r)

            def scale_body(i):
                for k in range(SLOTS):
                    a = tile_at(i, k, 0)
                    if a.there:
                        sp.wait_ge(x_scaled, a.no + 1)
                        if not (peeled(i) and a.no + SLOTS >= TILES):
                            load_x(a.no + SLOTS, k)
                        sp.dma_start(view(xs, a.no), agg_t[a.r][:, :, :]).then_inc(x_stored[a.r], 16)
            pipeline(sp, scale_body, 1, stop=TILES // SLOTS - 1)
            for r in range(SLOTS):
                sp.wait_ge(x_stored[r], load_base(1, r) // LOADS[0])

            for l in range(LAYERS):
                def load_agg(tile, q):
                    place = ah_t[q][:, :, 0:D] if l in GRU else agg_t[q][:, :, :]
                    sp.dma_start(place, view(agg, tile)).then_inc(loaded[q], 16)

                def load_state(tile, q):
                    if l in GRU:
                        sp.dma_start(ah_t[q][:, :, D:2 * D], view(layer_in[l], tile)).then_inc(loaded[q], 16)
                        sp.dma_start(aux_t[q][:, :, :], view(aux, tile)).then_inc(loaded[q], 16)
                    else:
                        h = hs_t[q] if l in WITH_S else h_t[q]
                        sp.dma_start(h[:, :, :], view(layer_in[l], tile)).then_inc(loaded[q], 16)
                        if l in SCALED:
                            load_s(tile, q, loaded[q])
                    if l == 1:
                        parts = LASTP if peeled(tile) and tile == TILES - 1 else P
                        sp.dma_start(res_t[q][0:parts, :, :], view(layer_res[l], tile, parts)).then_inc(loaded[q], 16)

                def store(tile, q):
                    parts = LASTP if peeled(tile) and tile == TILES - 1 and l == LAYERS - 1 else P
                    o = os_t if l + 1 in WITH_S else o_t
                    sp.dma_start(view(layer_out[l], tile, parts), o[q][0:parts, :, :]).then_inc(stored[q], 16)

                def load_residual(tile, r):
                    sp.dma_start(res_t[r][:, :, :], view(x2, tile)).then_inc(res_loaded[r], 16)
                    load_s(tile, r, res_loaded[r])

                for r in range(SLOTS):
                    load_state(r, r)
                if l == 4:
                    for r in range(SLOTS - 1):
                        load_residual(r, r)
                edge_pass(l)
                sp.wait_ge(c_scattered, 16 * C_ROWS * (carry_no(l) + 1))
                for r in range(SLOTS):
                    load_agg(r, r)

                def body(i):
                    for k in range(SLOTS):
                        a, b = tile_at(i, k, 0), tile_at(i, k, LAG[l])
                        if a.there:
                            if l == 0:
                                sp.wait_ge(finished, a.no + 1)
                            elif l in GRU:
                                sp.wait_ge(g_new, gru_base(l) + a.no * 2 + 2)
                            else:
                                sp.wait_ge(z_ready, ln_base(l) + a.no + 1)
                            if not (peeled(i) and a.no + SLOTS >= TILES):
                                load_agg(a.no + SLOTS, k)
                                load_state(a.no + SLOTS, k)
                            if l == 4 and not (peeled(i) and a.no + SLOTS - 1 >= TILES):
                                if not (peeled(i) and a.no < 1):
                                    sp.wait_ge(z_ready, ln_base(l) + a.no)
                                load_residual(a.no + SLOTS - 1, (k + SLOTS - 1) % SLOTS)
                        if b.there:
                            sp.wait_ge(finished, TILES * l + b.no + 1)
                            store(b.no, b.q)
                pipeline(sp, body, LAG[l], stop=TILES // SLOTS - 1)
                for q in range(2):
                    sp.wait_ge(stored[q], 16 * BT * (l + 1))

        @block.gpsimd
        def _(pool):
            nc.gpsimd.iota(cols_i[:, :], pattern=[[1, P]], base=0, channel_multiplier=0).then_inc(iotas, 1)
            nc.gpsimd.iota(part_i[:, :], pattern=[[0, 1]], base=0, channel_multiplier=1).then_inc(iotas, 1)
            for q in range(2):
                nc.gpsimd.memset(b_t[q][:, :, :], 1.0).then_inc(iotas, 1)
            for b in (h_t[(TILES - 1) % SLOTS], res_t[(TILES - 1) % SLOTS]):
                nc.gpsimd.memset(b[:, :, :], 0.0).then_inc(iotas, 1)
            pool.wait_ge(prep, 1)
            has_more = pool.value_load(more[0:1, 0:1], min_val=0, max_val=1)

            def gather_group(p, m, q, n):
                pool.wait_ge(src_staged[m][q], n + 1)
                pool.sem_inc(pool_turn, 1)
                w = DS if p in WITH_S else D
                for c in range(GC):
                    nc.gpsimd.indirect_dma_start(rows[q][:, c, 0:w], None, layer_in[p], bass.IndirectOffsetOnAxis(
                        ap=src_st[q][:, c:c + 1], axis=0)).then_inc(gathered[m][q], 16)

            def scatter_group(p, m, q, i):
                out, tab = (esums, aux) if p == "aux" else (sums, agg)
                n = edge_base(p) + i
                tab = tab[0:N, :].rearrange("(n a) d -> n (a d)", a=QN)
                pool.wait_ge(dst_staged[m][q], n + 1)
                pool.wait_ge(sums_out[m][q], n + 1)
                pool.sem_inc(pool_turn, 1)
                for c in range(GP):
                    src = out[q][:, c, :, :].rearrange("p a d -> p (a d)") if p == "aux" else out[q][:, c, :]
                    nc.gpsimd.indirect_dma_start(tab, bass.IndirectOffsetOnAxis(
                        ap=dst_st[q][:, c:c + 1], axis=0), src, None,
                        bounds_check=N // QN - 1, oob_is_err=False).then_inc(scattered[m][q], 16)

            def part(p, m):
                if p != "aux":
                    for q in range(SL):
                        gather_group(p, m, q, gather_base(p))

                def body(i):
                    for q in range(SL):
                        scatter_group(p, m, q, i)
                        if p != "aux" and not (peeled(i) and i == STEPS - 1):
                            gather_group(p, m, q, gather_base(p) + i + 1)
                walk(pool, STEPS, body)

            def carry_stage(p):
                old, new, tab = (cold_aux, cnew_aux, aux) if p == "aux" else (cold, cnew, agg)
                for q in range(SL):
                    pool.wait_ge(scattered[0][q], 16 * GP * (edge_base(p) + STEPS))
                tab = tab[0:N, :].rearrange("(n a) d -> n (a d)", a=QN)
                for b in range(CB):
                    nc.gpsimd.indirect_dma_start(old[:, b, :], None, tab, bass.IndirectOffsetOnAxis(
                        ap=carry_src[:, b:b + 1], axis=0), bounds_check=N // QN - 1, oob_is_err=False
                        ).then_inc(c_gathered, 16)
                pool.wait_ge(c_added, carry_no(p) + 1)
                for b in range(CB):
                    nc.gpsimd.indirect_dma_start(tab, bass.IndirectOffsetOnAxis(
                        ap=carry_dst[:, b:b + 1], axis=0), new[:, b, :], None,
                        bounds_check=N // QN - 1, oob_is_err=False).then_inc(c_scattered, 16)

            pool.wait_ge(aux_zeroed, 16 * 8)
            both_parts(pool, has_more, "aux", part)
            carry_stage("aux")

            pool.wait_ge(agg_zeroed, 16 * STEPS)
            for l in range(LAYERS):
                if l == 0:
                    for r in range(SLOTS):
                        pool.wait_ge(x_stored[r], load_base(1, r) // LOADS[0])
                else:
                    for q in range(2):
                        pool.wait_ge(stored[q], 16 * BT * l)
                both_parts(pool, has_more, l, part)
                carry_stage(l)

                if l in GRU:
                    def operand(a):
                        q = a.q
                        pool.wait_ge(loaded[a.r], load_base(l, a.r) + (a.step + 1) * (16 * LOADS[l]))
                        if not a.early:
                            pool.wait_ge(g_transposed, gru_base(l) + a.no * 2 - 2)
                        nc.gpsimd.tensor_tensor(b_t[q][:, :, 0:D], ah_t[a.r][:, :, D:2 * D],
                                                aux_t[a.r][:, :, DE:AW].to_broadcast([P, NPP, D]),
                                                ALU.mult).then_inc(b_ready, 1)
                        nc.gpsimd.tensor_copy(b_t[q][:, :, D:D + AW], aux_t[a.r][:, :, :]).then_inc(b_ready, 1)

                    def new_state(u):
                        n, g, q = gru_base(l) + u.no, u.g, u.tile.q
                        half = slice(g * HN, (g + 1) * HN)
                        out = z_t if l in LN else o_t
                        pool.wait_ge(n_act, n + 1)
                        nc.gpsimd.tensor_tensor(d_t[g][:, :, :], ah_t[u.tile.r][:, half, D:2 * D], n_t[g][:, :, :],
                                                ALU.subtract).then_inc(g_diff, 1)
                        pool.wait_ge(g_diff, n + 1)
                        nc.gpsimd.tensor_tensor(m_t[g][:, :, :], d_t[g][:, :, :], rz_t[g][:, :, D:2 * D],
                                                ALU.mult).then_inc(g_scaled, 1)
                        if g == 0 and not u.tile.early:
                            if l in LN:
                                pool.wait_ge(n_centred, ln_base(l) + u.tile.no - 1)
                            else:
                                pool.wait_ge(stored[q], 16 * BT * l + u.tile.pair * 16)
                        pool.wait_ge(g_scaled, n + 1)
                        ins = nc.gpsimd.tensor_tensor(out[q][:, half, :], m_t[g][:, :, :], n_t[g][:, :, :], ALU.add)
                        ins.then_inc(g_new, 1)
                        if l not in LN and g == 1:
                            pool.wait_ge(g_new, n + 1)
                            pool.sem_inc(finished, 1)

                    operand(Tile(0, 0))

                    def body(i):
                        for k in range(2 * SLOTS):
                            if k % 2 == 0:
                                a = tile_at(i, k // 2, -1)
                                if a.there:
                                    operand(a)
                            u = unit_at(i, k, 2)
                            if u.there:
                                new_state(u)
                    pipeline(pool, body, 1)
                else:
                    def body(i):
                        for k in range(SLOTS):
                            a = tile_at(i, k, 0)
                            if not a.there:
                                continue
                            n, q, r = gcn_base(l) + a.no, a.q, a.r
                            pool.wait_ge(loaded[r], load_base(l, r) + (a.step + 1) * (16 * LOADS[l]))
                            if l in WITH_S:
                                s_b = hs_t[r][:, :, D:DS].to_broadcast([P, NPP, D])
                                nc.gpsimd.tensor_tensor(y0_t[q][:, :, :], hs_t[r][:, :, 0:D], s_b, ALU.mult
                                                        ).then_inc(y_scaled, 1)
                                pool.wait_ge(y_scaled, TILES * WITH_S.index(l) + a.no + 1)
                                scaled = y0_t[q]
                            else:
                                s_b = s_t[r][:, :].rearrange("p (j a) -> p j a", a=1).to_broadcast([P, NPP, D])
                                scaled = h_t[r]
                            nc.gpsimd.tensor_tensor(y1_t[q][:, :, :], scaled[:, :, :], agg_t[r][:, :, :], ALU.add
                                                    ).then_inc(y_summed, 1)
                            if not a.early:
                                pool.wait_ge(y_transposed, n - 1)
                            pool.wait_ge(y_summed, n + 1)
                            nc.gpsimd.tensor_tensor(y_t[q][:, :, :], y1_t[q][:, :, :], s_b, ALU.mult
                                                    ).then_inc(y_ready, 1)
                    pipeline(pool, body, 1)

        @block.scalar
        def _(act):
            act.wait_ge(prep, 1)
            has_more = act.value_load(more[0:1, 0:1], min_val=0, max_val=1)

            def clear(i):
                count = min(ZR, NPAD // P - i * ZR) if peeled(i) else ZR
                nc.scalar.dma_start(agg.rearrange("(p k) d -> p (k d)", p=P)[:, bass.ds(i * (ZR * D), count * D)],
                                    zeros[:, 0:count * D]).then_inc(agg_zeroed, 16)

            def part(p, m):
                def body(i):
                    if p == "aux" and m == 0:
                        clear(i)
                    for q in range(SL):
                        n = edge_base(p) + i
                        if not (p == "aux" and peeled(i) and i == 0):
                            act.wait_ge(scattered[m][q], n * (16 * GP))
                            if m == 0:
                                act.wait_ge(carried[q], n * 16)
                        if p == "aux":
                            act.wait_ge(marks_out[m][q], i + 1)
                            for c in range(GP):
                                ins = nc.scalar.copy(esums[q][:, c, :, :], psS[q][c][:, 0:QN * EW]
                                                     .rearrange("p (a d) -> p a d", d=EW)[:, :, 0:AW])
                        else:
                            act.wait_ge(combined[m][q], n + 1)
                            for c in range(GP):
                                ins = nc.scalar.copy(sums[q][:, c, :], psS[q][c][:, 0:QN * D])
                        ins.then_inc(sums_out[m][q], 1)
                walk(act, STEPS, body)

            def edge_pass(p):
                both_parts(act, has_more, p, part)

            edge_pass("aux")
            act.wait_ge(eps_set, 1)
            act.wait_ge(s_done, 8)
            nc.scalar.activation(deg[:, :], deg[:, :], ACT.Sqrt).then_inc(deg_root, 1)
            for l in range(LAYERS):
                edge_pass(l)

                def square(a):
                    if a.there:
                        n = ln_base(l) + a.no
                        act.wait_ge(n_centred, n + 1)
                        if not a.early:
                            act.wait_ge(n_var, n - 1)
                        nc.scalar.activation(sq_t[a.q][:, :, :], xc_t[a.q][:, :, :], ACT.Square
                                             ).then_inc(n_squared, 1)

                def root(a):
                    if a.there:
                        n = ln_base(l) + a.no
                        act.wait_ge(n_var, n + 1)
                        nc.scalar.activation(st_t[a.q][:, 3, :], st_t[a.q][:, 2, :], ACT.Sqrt,
                                             bias=eps[:, 0:1], scale=1.0 / D).then_inc(n_std, 1)

                if l in GRU:
                    def body(i):
                        for k in range(2 * SLOTS):
                            u = unit_at(i, k, 0)
                            if u.there:
                                act.wait_ge(g_transposed, gru_base(l) + u.no + 1)
                                if not u.early:
                                    act.wait_ge(g_mm, gru_base(l) + u.no - 1)
                                nc.scalar.copy(aT[u.g][:, :], psA[u.g][:, :])
                                nc.scalar.copy(bT[u.g][:, :], psB[u.g][0:KB, :]).then_inc(ops_ready, 1)
                            u = unit_at(i, k, 1)
                            if u.there:
                                act.wait_ge(g_mm, gru_base(l) + u.no + 1)
                                if not u.early:
                                    act.wait_ge(g_scaled, gru_base(l) + u.no - 1)
                                nc.scalar.activation(rz_t[u.g][:, :, :], psG[u.g][:, :, 0:2 * D], ACT.Sigmoid
                                                     ).then_inc(gates, 1)
                            u = unit_at(i, k, 2)
                            if u.there:
                                act.wait_ge(n_pre, gru_base(l) + u.no + 1)
                                if not u.early:
                                    act.wait_ge(g_new, gru_base(l) + u.no - 1)
                                nc.scalar.activation(n_t[u.g][:, :, :], d2_t[u.g][:, :, :], ACT.Tanh
                                                     ).then_inc(n_act, 1)
                            if l in LN and k % 2 == 0:
                                square(tile_at(i, k // 2, 3))
                    pipeline(act, body, 3)
                else:
                    def body(i):
                        for k in range(SLOTS):
                            a = tile_at(i, k, 0)
                            if a.there:
                                act.wait_ge(y_transposed, gcn_base(l) + a.no + 1)
                                if not a.early:
                                    act.wait_ge(mm_done, gcn_base(l) + a.no - 1)
                                nc.scalar.copy(yT[a.q][:, :], psA[a.q][:, :]).then_inc(yT_ready, 1)
                            if l:
                                a = tile_at(i, k, 1)
                                if l == 2 and a.there:
                                    act.wait_ge(mm_done, gcn_base(l) + a.no + 1)
                                    if not a.early:
                                        act.wait_ge(z_acted, a.no - 1)
                                    nc.scalar.copy(za_t[a.q][:, :, :], psB[a.q][:, :]
                                                   .rearrange("p (j d) -> p j d", d=D)).then_inc(z_copied, 1)
                                square(tile_at(i, k, 2 if l == 2 else 1))
                                root(tile_at(i, k, 3 if l == 2 else 2))
                    pipeline(act, body, 3 if l == 2 else 2)

        @block.vector
        def _(dve):
            V = nc.vector
            for l in range(4):
                ins = V.memset(BW[l][:, :], 0.0)
            for r in range(2):
                ins = V.memset(RA[r][:, :], 0.0)
            ins.then_inc(bw_zeroed, 1)
            V.memset(zeros[:, :], 0.0).then_inc(zeros_set, 1)
            V.memset(eps[:, :], EPS).then_inc(eps_set, 1)
            V.memset(cbuf[:, :, :], 0.0)
            V.memset(cbuf_aux[:, :, :], 0.0)
            V.memset(cold[:, :, :], 0.0)
            V.memset(cold_aux[:, :, :], 0.0)
            for r in range(2):
                V.memset(RB[r][:, :], 0.0)
            for q in range(SL):
                V.memset(erows[q][:, :, :], 1.0)
            steps = [0]

            def link(ins):
                steps[0] += 1
                ins.then_inc(prep_w, 1)
                dve.wait_ge(prep_w, steps[0])

            dve.wait_ge(iotas, 6)
            V.tensor_copy(cols[:, :], cols_i[:, :])
            link(V.tensor_copy(part[:, :], part_i[:, :]))
            V.tensor_scalar(ident[:, :], cols[:, 0:P], part[:, 0:1], None, ALU.is_equal)
            dve.wait_ge(in_loaded, 16 * PREP_LOADS)
            flat = "p a b -> p (a b)"

            def block_of(dst, src):
                link(V.tensor_copy(dst, src))
                link(V.tensor_scalar(dst, dst, 1.0 / QN, -(QN - 1) / (2.0 * QN), ALU.mult, ALU.add))
                link(V.tensor_scalar(dst, dst, ROUND, None, ALU.add))
                link(V.tensor_scalar(dst, dst, -ROUND, None, ALU.add))

            block_of(blk[:, :, :].rearrange(flat), dst_r[:, :])
            block_of(prv_block[:, :, :].rearrange(flat), prv_r[:, :])
            block_of(back_block[:, :], back_r[:, :])
            block_of(head_block[:, :], head_r[:, :])
            link(V.tensor_copy(dst_f, dst_r[:, :]))
            link(V.scalar_tensor_tensor(node[:, :, :].rearrange(flat), blk[:, :, :].rearrange(flat), -float(QN),
                                        dst_f, ALU.mult, ALU.add))
            link(V.tensor_tensor(begin[:, :, :], blk[:, :, :], prv_block[:, :, :], ALU.not_equal))
            left = bias
            for k in range(3):
                link(V.tensor_copy(bias_part[k][:, :, :], left[:, :, :]))
                if k < 2:
                    link(V.tensor_tensor(bias_left[k][:, :, :], left[:, :, :], bias_part[k][:, :, :], ALU.subtract))
                    left = bias_left[k]
            link(V.tensor_scalar(bias_left[0][:, :, :], bias_part[0][:, :, :], ident[:, 0:1], None, ALU.mult))
            link(V.scalar_tensor_tensor(bias_left[1][:, :, :], bias_part[1][:, :, :], ident[:, 1:2],
                                        bias_left[0][:, :, :], ALU.mult, ALU.add))
            link(V.scalar_tensor_tensor(bias_left[0][:, :, :], bias_part[2][:, :, :], ident[:, 2:3],
                                        bias_left[1][:, :, :], ALU.mult, ALU.add))
            for l in range(4):
                V.tensor_copy(bias_rows3[l][:, :, :], bias_left[0][:, l:l + 1, :].to_broadcast([P, NPP, D]))
            V.memset(ones3[:, :], 1.0)
            V.memset(rank[0][:, :, 0:1], 0.0)
            link(V.tensor_copy(rank[0][:, :, 1:EP], begin[:, :, 1:EP]))
            k, a = 1, 0
            while k < EP:
                V.tensor_copy(rank[1 - a][:, :, 0:k], rank[a][:, :, 0:k])
                link(V.tensor_tensor(rank[1 - a][:, :, k:EP], rank[a][:, :, k:EP], rank[a][:, :, 0:EP - k], ALU.add))
                k, a = 2 * k, 1 - a
            link(V.tensor_scalar(high, rank[a][:, :, EP - 1], float(P), None, ALU.is_ge))
            link(V.scalar_tensor_tensor(block_mark[:, :, :], blk[:, :, :], -FAR, begin[:, :, :], ALU.add, ALU.mult))
            link(V.tensor_scalar(cont[:, :], begin[:, :, 0], -1.0, 1.0, ALU.mult, ALU.add))
            link(V.tensor_tensor(lead[:, :], back_block[:, :], blk[:, :, 0], ALU.not_equal))
            link(V.tensor_tensor(cidx_f[:, :], lead[:, :], cont[:, :], ALU.mult))
            link(V.tensor_scalar(lead[:, :], cidx_f[:, :], -FAR, FAR, ALU.mult, ALU.add))
            link(V.tensor_tensor(cidx_f[:, :], lead[:, :], blk[:, :, 0], ALU.add))
            V.tensor_copy(carry_dst[:, :], cidx_f[:, :])
            V.tensor_copy(carry_src[:, :], blk[:, :, 0])
            for b in range(CB):
                ins = V.tensor_scalar(same[:, b, :], head_block[:, :], blk[:, b, 0:1], cont[:, b:b + 1], ALU.is_equal,
                                      ALU.mult)
            ins.then_inc(prep_t, 1)
            dve.wait_ge(fold_mm, 1)

            def by_chunk(ps, width):
                v = ps[:, :].rearrange("p (b h i) -> p b i h", b=CB, h=2)
                return [(b, v[:, b, 0:min(P, width // 2 - b * P), :]) for b in range(CB)]

            for ps, dst in ((psA[0], rank_c[0][:, :]), (psB[0], mark_c[:, :, 0])):
                for b, v in by_chunk(ps, CHUNKS):
                    out = dst[:, b * EP:b * EP + 2 * v.shape[1]].rearrange("p (i h) -> p i h", h=2)
                    V.tensor_copy(out, v)
            for b, v in by_chunk(psA[0], CHUNKS):
                out = rank_c[1][:, b * EP:b * EP + 2 * v.shape[1]].rearrange("p (i h) -> p i h", h=2)
                V.tensor_scalar(out, v, -float(P), None, ALU.add)
            for a in range(QN):
                for b, v in by_chunk(psA[1], CHUNKS):
                    out = node_c[:, b * EP:b * EP + 2 * v.shape[1], a].rearrange("p (i h) -> p i h", h=2)
                    V.tensor_scalar(out, v, float(a), None, ALU.is_equal)
            link(V.tensor_reduce(any_high, psG[0][0:1, 0, 0:CB * P], AX.X, ALU.max))
            V.tensor_copy(more[0:1, 0:1], any_high).then_inc(prep, 1)
            dve.wait_ge(prep, 1)
            has_more = dve.value_load(more[0:1, 0:1], min_val=0, max_val=1)
            dve.wait_ge(fold_mm, 2)
            for r in range(2):
                V.tensor_copy(RA[r][0:D, 0:3 * D], psB[0][0:D, r * 3 * D:(r + 1) * 3 * D])
                ins = V.tensor_copy(RB[r][0:D + AW, 0:3 * D], psB[1][0:D + AW, r * 3 * D:(r + 1) * 3 * D])
            ins.then_inc(ones_set, 1)

            def stage_src(m, q, i, n):
                if not (peeled(i) and i == 0 and n == 0):
                    dve.wait_ge(gathered[m][q], n * (16 * GC))
                V.tensor_copy(src_st[q][:, :], src_c[:, bass.ds((i * SL + q) * GC, GC)]).then_inc(src_staged[m][q], 1)

            def selection(p, m, q, i):
                for c in range(GC):
                    e = bass.ds((i * SL + q) * GC + c, 1)
                    if p in WITH_S:
                        V.tensor_scalar(sel[q][:, c, :], cols[:, :], rank_c[m][:, e], rows[q][:, c, D:DS], ALU.is_equal,
                                        ALU.mult)
                    else:
                        V.tensor_scalar(sel[q][:, c, :], cols[:, :], rank_c[m][:, e], None, ALU.is_equal)

            def spread_over_block(dst, src, q, i):
                places = node_c[:, bass.ds((i * SL + q) * GC, GC), :].rearrange("p c (a o) -> p c a o", o=1)
                w = src.shape[2]
                return V.tensor_tensor(dst, src.rearrange("p c (o d) -> p c o d", o=1).to_broadcast([P, GC, QN, w]),
                                       places.to_broadcast([P, GC, QN, w]), ALU.mult)

            def layer_part(p, m):
                for q in range(SL):
                    stage_src(m, q, 0, gather_base(p))

                def body(i):
                    for q in range(SL):
                        n, g = edge_base(p) + i, gather_base(p) + i
                        dve.wait_ge(combined[m][q], n)
                        if p not in WITH_S:
                            selection(p, m, q, i)
                        dve.wait_ge(scattered[m][q], n * (16 * GP))
                        V.tensor_copy(dst_st[q][:, :], dst_idx[m][:, bass.ds((i * SL + q) * GP, GP)]
                                      ).then_inc(dst_staged[m][q], 1)
                        dve.wait_ge(gathered[m][q], (g + 1) * (16 * GC))
                        if p in WITH_S:
                            selection(p, m, q, i)
                        spread_over_block(srows[q], rows[q][:, :, 0:D], q, i).then_inc(spread_out[m][q], 1)
                        if not (peeled(i) and i == STEPS - 1):
                            stage_src(m, q, i + 1, g + 1)
                walk(dve, STEPS, body)

            def aux_part(p, m):
                def take_marks(q, i):
                    dve.wait_ge(combined[m][q], i + 1)
                    for c in range(GP):
                        ins = V.tensor_reduce(marks[q][:, c:c + 1], psS[q][c][:, 0:QN * EW]
                                              .rearrange("p (a d) -> p d a", d=EW)[:, AW:EW, :], AX.X, ALU.add)
                    ins.then_inc(marks_out[m][q], 1)
                    if not (peeled(i) and i == 0):
                        dve.wait_ge(scattered[m][q], i * (16 * GP))
                    dve.wait_ge(marks_out[m][q], i + 1)
                    V.tensor_scalar(dst_st[q][:, :], marks[q][:, :], FAR, None, ALU.add).then_inc(dst_staged[m][q], 1)
                    V.tensor_scalar(dst_idx[m][:, bass.ds((i * SL + q) * GP, GP)], marks[q][:, :], FAR, None, ALU.add
                                    ).then_inc(idx_set[m][q], 1)

                def body(i):
                    for q in range(SL):
                        if not (peeled(i) and i == 0):
                            dve.wait_ge(combined[m][q], i)
                        selection(p, m, q, i)
                        spread_over_block(esrows[q][:, :, :, AW:EW], mark_c[:, bass.ds((i * SL + q) * GC, GC), :], q, i)
                        dve.wait_ge(e_loaded[m][q], (i + 1) * 16)
                        spread_over_block(esrows[q][:, :, :, 0:AW], erows[q][:, :, :], q, i
                                          ).then_inc(spread_out[m][q], 1)
                        if q:
                            take_marks(q - 1, i)
                        elif not (peeled(i) and i == 0):
                            take_marks(SL - 1, i - 1)
                walk(dve, STEPS, body)
                take_marks(SL - 1, STEPS - 1)
                for q in range(SL):
                    dve.wait_ge(idx_set[m][q], STEPS)

            def edge_pass(p):
                both_parts(dve, has_more, p, aux_part if p == "aux" else layer_part)
                old, new, w = (cold_aux, cnew_aux, AW) if p == "aux" else (cold, cnew, D)
                dve.wait_ge(c_combined, carry_no(p) + 1)
                dve.wait_ge(c_gathered, 16 * C_ROWS * (carry_no(p) + 1))
                for b in range(CB):
                    ins = V.tensor_tensor(new[:, b, :], old[:, b, :], psB[b][:, 0:QN * w], ALU.add)
                ins.then_inc(c_added, 1)

            edge_pass("aux")
            for k in range(8):
                dve.wait_ge(aux_loaded[k % 3], 16 * (k // 3 + 1))
                V.tensor_scalar(deg[:, k * WB:(k + 1) * WB],
                                piece[k % 3].rearrange("p (k d) -> p k d", d=AW)[:, :, DE],
                                1.0, None, ALU.add).then_inc(s_done, 1)
            dve.wait_ge(deg_root, 1)
            V.reciprocal(s_big[:, :], deg[:, :]).then_inc(s_ready, 1)

            def scale_body(i):
                for k in range(SLOTS):
                    a = tile_at(i, k, 0)
                    if a.there:
                        dve.wait_ge(x_loaded[a.r], (a.step + 1) * 32)
                        if not peeled(a.step) or a.step:
                            dve.wait_ge(x_stored[a.r], a.step * 16)
                        V.tensor_tensor(agg_t[a.r][:, :, :], h_t[a.r][:, :, :], s_t[a.r][:, :]
                                        .rearrange("p (j a) -> p j a", a=1).to_broadcast([P, NPP, D]), ALU.mult
                                        ).then_inc(x_scaled, 1)
            pipeline(dve, scale_body, 1)

            def keep_s(a):
                V.tensor_copy(s_keep[a.r][:, :], s_t[a.r][:, :])

            def centre(l, a):
                n, z, st = ln_base(l) + a.no, z_t[a.q], st_t[a.q]
                dve.wait_ge(z_ready, n + 1)
                V.tensor_reduce(st[:, 0, :], z[:, :, :], AX.X, ALU.add).then_inc(n_sum, 1)
                dve.wait_ge(n_sum, n + 1)
                V.scalar_tensor_tensor(xc_t[a.q][:, :, :], st[:, 0, :].rearrange("p (j a) -> p j a", a=1)
                                       .to_broadcast([P, NPP, D]), -1.0 / D, z[:, :, :], ALU.mult, ALU.add
                                       ).then_inc(n_centred, 1)

            def variance(l, a):
                n = ln_base(l) + a.no
                dve.wait_ge(n_squared, n + 1)
                V.tensor_reduce(st_t[a.q][:, 2, :], sq_t[a.q][:, :, :], AX.X, ALU.add).then_inc(n_var, 1)

            def inverse_root(l, a):
                st, k = st_t[a.q], [0]
                v, y, u = st[:, 3, :], st[:, 1, :], st[:, 4, :]

                def link(ins):
                    k[0] += 1
                    ins.then_inc(newton, 1)
                    dve.wait_ge(newton, a.no * NEWTON + k[0])

                dve.wait_ge(n_var, ln_base(l) + a.no + 1)
                link(V.tensor_scalar(v, st[:, 2, :], 1.0 / D, EPS, ALU.mult, ALU.add))
                link(V.tensor_scalar(u.bitcast(i32), v.bitcast(i32), 1, None, ALU.arith_shift_right))
                link(V.tensor_scalar(y.bitcast(i32), u.bitcast(i32), -1.0, float(0x5f3759df), ALU.mult, ALU.add))
                for _ in range(3):
                    link(V.tensor_tensor(u, y, y, ALU.mult))
                    link(V.scalar_tensor_tensor(st[:, 5, :], u, -0.5, v, ALU.mult, ALU.mult))
                    link(V.scalar_tensor_tensor(y, st[:, 5, :], 1.5, y, ALU.add, ALU.mult))

            def normalise(l, a):
                n, st = ln_base(l) + a.no, st_t[a.q]
                if l not in GRU:
                    dve.wait_ge(n_std, n_std_base(l) + a.no + 1)
                    V.reciprocal(st[:, 1, :], st[:, 3, :]).then_inc(n_rstd, 1)
                    dve.wait_ge(n_rstd, n_std_base(l) + a.no + 1)
                if not a.early:
                    dve.wait_ge(stored[a.q], 16 * BT * l + a.pair * 16)
                o = o_t[a.q]
                if l + 1 in WITH_S:
                    o = os_t[a.q][:, :, 0:D]
                    V.tensor_copy(os_t[a.q][:, :, D], s_keep[a.r][:, :])
                V.tensor_tensor(o, xc_t[a.q][:, :, :], st[:, 1, :].rearrange("p (j a) -> p j a", a=1)
                                .to_broadcast([P, NPP, D]), ALU.mult).then_inc(finished, 1)

            for l in range(LAYERS):
                edge_pass(l)
                if l in GRU:
                    def body(i):
                        for k in range(2 * SLOTS):
                            u = unit_at(i, k, 1)
                            if u.there:
                                n = gru_base(l) + u.no
                                dve.wait_ge(gates, n + 1)
                                V.tensor_tensor(d3_t[u.g][:, :, :], rz_t[u.g][:, :, 0:D], psG[u.g][:, :, 3 * D:GW],
                                                ALU.mult).then_inc(n_prod, 1)
                                if not u.early:
                                    dve.wait_ge(n_act, n - 1)
                                dve.wait_ge(n_prod, n + 1)
                                V.tensor_tensor(d2_t[u.g][:, :, :], d3_t[u.g][:, :, :], psG[u.g][:, :, 2 * D:3 * D],
                                                ALU.add).then_inc(n_pre, 1)
                            if l in LN and k % 2 == 0:
                                c = tile_at(i, k // 2, 4)
                                if c.there:
                                    inverse_root(l, c)
                                    normalise(l, c)
                            if l in LN and k % 2 == 1:
                                a, b = (tile_at(i, k // 2, lag) for lag in (2, 3))
                                if a.there:
                                    dve.wait_ge(g_new, gru_base(l) + a.no * 2 + 2)
                                    dve.wait_ge(res_loaded[a.r], (a.step + 1) * 32)
                                    keep_s(a)
                                    V.tensor_tensor(z_t[a.q][:, :, :], z_t[a.q][:, :, :], res_t[a.r][:, :, :],
                                                    ALU.add).then_inc(z_ready, 1)
                                    centre(l, a)
                                if b.there:
                                    variance(l, b)
                    pipeline(dve, body, 4)
                elif l == 0:
                    def body(i):
                        for k in range(SLOTS):
                            a = tile_at(i, k, 0)
                            if a.there:
                                dve.wait_ge(mm_done, a.no + 1)
                                if not a.early:
                                    dve.wait_ge(stored[a.q], a.pair * 16)
                                V.scalar_tensor_tensor(o_t[a.q][:, :, :], psB[a.q][:, :]
                                                       .rearrange("p (j d) -> p j d", d=D), 0.0, s_t[a.r][:, :]
                                                       .rearrange("p (j a) -> p j a", a=1)
                                                       .to_broadcast([P, NPP, D]), ALU.max, ALU.mult
                                                       ).then_inc(finished, 1)
                    pipeline(dve, body, 1)
                else:
                    def body(i):
                        for k in range(SLOTS):
                            a, b, c = (tile_at(i, k, lag) for lag in (0, 1, 2))
                            q = a.q
                            z, product = z_t[q], psB[q][:, :].rearrange("p (j d) -> p j d", d=D)
                            if a.there:
                                if l == 2:
                                    dve.wait_ge(z_copied, a.no + 1)
                                else:
                                    dve.wait_ge(mm_done, gcn_base(l) + a.no + 1)
                                if l == 1:
                                    dve.wait_ge(loaded[a.r], load_base(l, a.r) + (a.step + 1) * (16 * LOADS[l]))
                                    keep_s(a)
                                    V.tensor_tensor(z[:, :, :], product, res_t[a.r][:, :, :], ALU.add
                                                    ).then_inc(z_ready, 1)
                                elif l == 2:
                                    zc = za_t[q]
                                    V.scalar_tensor_tensor(z2_t[q][:, :, :], zc[:, :, :], 0.1, zc[:, :, :],
                                                           ALU.mult, ALU.max).then_inc(z_acted, 1)
                                    dve.wait_ge(z_acted, a.no + 1)
                                    V.tensor_tensor(z[:, :, :], z2_t[q][:, :, :], hs_t[a.r][:, :, 0:D], ALU.add
                                                    ).then_inc(z_ready, 1)
                                else:
                                    V.scalar_tensor_tensor(z[:, :, :], product, 0.0, hs_t[a.r][:, :, 0:D], ALU.max,
                                                           ALU.add).then_inc(z_ready, 1)
                            if c.there:
                                normalise(l, c)
                            if a.there:
                                centre(l, a)
                            if b.there:
                                variance(l, b)
                    pipeline(dve, body, 2)

        @block.tensor
        def _(pe):
            pe.wait_ge(prep_t, 1)
            for tab, ps in ((rank[0], psA[0]), (node, psA[1]), (block_mark, psB[0])):
                for b in range(CB):
                    for h in range(2):
                        nc.tensor.transpose(ps[:, (2 * b + h) * P:(2 * b + h + 1) * P],
                                            tab[:, b, h * P:(h + 1) * P], ident[:, :])
            for b in range(CB):
                ins = nc.tensor.transpose(psG[0][0:1, 0, b * P:(b + 1) * P], high[:, b:b + 1], ident[:, :])
            ins.then_inc(fold_mm, 1)
            pe.wait_ge(prep, 1)
            has_more = pe.value_load(more[0:1, 0:1], min_val=0, max_val=1)
            for r in range(2):
                c = slice(r * 3 * D, (r + 1) * 3 * D)
                nc.tensor.matmul(psB[0][0:D, c], wms[r][:, :], wih[r][:, :], start=True, stop=True)
                ins = nc.tensor.matmul(psB[1][0:D + AW, c], wmd[r][:, :], wih[r][:, :], start=True, stop=True)
            ins.then_inc(fold_mm, 1)
            pe.wait_ge(ones_set, 1)
            pe.wait_ge(bias_rows, 32)
            pe.wait_ge(bw_loaded, 16 * 12)

            def part(p, m):
                src, w = (esrows, QN * EW) if p == "aux" else (srows, QN * D)

                def body(i):
                    for q in range(SL):
                        n = edge_base(p) + i
                        pe.wait_ge(spread_out[m][q], n + 1)
                        if not (p == "aux" and peeled(i) and i == 0):
                            pe.wait_ge(sums_out[m][q], n)
                        for c in range(GP):
                            for h in range(2):
                                ins = nc.tensor.matmul(psS[q][c][:, 0:w], sel[q][:, 2 * c + h, :],
                                                       src[q][:, 2 * c + h, :, :].rearrange("p a d -> p (a d)"),
                                                       start=(h == 0), stop=(h == 1))
                        ins.then_inc(combined[m][q], 1)
                walk(pe, STEPS, body)

            def edge_pass(p):
                both_parts(pe, has_more, p, part)
                pe.wait_ge(c_loaded, 32 * (carry_no(p) + 1))
                cb, w = (cbuf_aux, QN * AW) if p == "aux" else (cbuf, QN * D)
                for b in range(CB):
                    for k in range(CB):
                        ins = nc.tensor.matmul(psB[b][:, 0:w], same[:, k, b * P:(b + 1) * P],
                                               cb[:, k, :], start=(k == 0), stop=(k == CB - 1))
                ins.then_inc(c_combined, 1)

            edge_pass("aux")
            for l in range(LAYERS):
                edge_pass(l)
                if l in GRU:
                    r = GRU.index(l)

                    def body(i):
                        for k in range(2 * SLOTS):
                            u = unit_at(i, k, 0)
                            if u.there:
                                q, r4, g, n = u.tile.q, u.tile.r, u.g, gru_base(l) + u.no
                                if g == 0:
                                    pe.wait_ge(loaded[r4], load_base(l, r4) + (u.tile.step + 1) * (16 * LOADS[l]))
                                    pe.wait_ge(b_ready, gru_base(l) + u.no + 2)
                                if not u.early:
                                    pe.wait_ge(ops_ready, n - 1)
                                for j in range(HN):
                                    nc.tensor.transpose(psA[g][:, j * P:(j + 1) * P], ah_t[r4][:, g * HN + j, :],
                                                        ident[:, :])
                                    ins = nc.tensor.transpose(psB[g][0:KB, j * P:(j + 1) * P],
                                                              b_t[q][:, g * HN + j, :], ident[:, :])
                                ins.then_inc(g_transposed, 1)
                            u = unit_at(i, k, 1)
                            if u.there:
                                g, n = u.g, gru_base(l) + u.no
                                pe.wait_ge(ops_ready, n + 1)
                                if not u.early:
                                    pe.wait_ge(n_pre, n - 1)
                                for j in range(HN):
                                    nc.tensor.matmul(psG[g][:, j, :], aT[g][:, j * P:(j + 1) * P], RA[r][:, :],
                                                     start=True, stop=False)
                                    ins = nc.tensor.matmul(psG[g][:, j, :], bT[g][:, j * P:(j + 1) * P],
                                                           RB[r][:, :], start=False, stop=True)
                                ins.then_inc(g_mm, 1)
                    pipeline(pe, body, 1)
                else:
                    w = {0: 0, 1: 1, 2: 2, 5: 3}[l]

                    def body(i):
                        for k in range(SLOTS):
                            a, b = tile_at(i, k, 0), tile_at(i, k, 1)
                            if a.there:
                                n, q = gcn_base(l) + a.no, a.q
                                pe.wait_ge(y_ready, n + 1)
                                if not a.early:
                                    pe.wait_ge(yT_ready, n - 1)
                                for j in range(NPP // 2):
                                    ins = nc.tensor.transpose(psA[q][:, j * P:(j + 1) * P],
                                                              y_t[q][:, 2 * j:2 * j + 2, :]
                                                              .rearrange("p a d -> p (a d)"), ident[:, :])
                                ins.then_inc(y_transposed, 1)
                            if b.there:
                                n = gcn_base(l) + b.no
                                pe.wait_ge(yT_ready, n + 1)
                                if not b.early:
                                    if l == 0:
                                        pe.wait_ge(finished, b.no - 1)
                                    elif l == 2:
                                        pe.wait_ge(z_copied, b.no - 1)
                                    else:
                                        pe.wait_ge(z_ready, ln_base(l) + b.no - 1)
                                nc.tensor.matmul(psB[b.q][:, :], ones3[:, :], bias_rows3[w][0:3, :, :]
                                                 .rearrange("p j d -> p (j d)"), start=True, stop=False)
                                for j in range(NPP // 2):
                                    ins = nc.tensor.matmul(psB[b.q][:, j * P:(j + 1) * P],
                                                           yT[b.q][:, j * P:(j + 1) * P], BW[w][:, :],
                                                           start=False, stop=(j == NPP // 2 - 1))
                                ins.then_inc(mm_done, 1)
                    pipeline(pe, body, 1)


def kernel(**inputs):
    import numpy as np
    import concourse.bacc as bacc
    from concourse.bass_utils import run_bass_kernel_spmd as run

    g = {k: np.asarray(v) for k, v in inputs.items()}
    pad = CB * P * EP
    src = np.concatenate([g["src"], np.zeros(CHUNKS * P - E, np.int32)])
    dst = np.concatenate([g["dst"], np.full(pad - E, N, np.int32)])
    before = np.concatenate([np.full(EP + 1, -QN, np.int32), dst])

    def by_pair(a):
        return a.reshape(CB, P, EP).transpose(1, 0, 2).reshape(P, CB * EP)

    arrays = {
        "x": g["x"],
        "edges": np.concatenate([g["edge_attr_16"], np.zeros((CHUNKS * P - E, DE), np.float32)]),
        "src_cols": src.reshape(CHUNKS, P).T,
        "dst_rows": by_pair(dst),
        "prev_rows": by_pair(before[EP:EP + pad]),
        "back": before[0:pad:EP].reshape(CB, P).T,
        "head": np.broadcast_to(dst[0:pad:EP], (P, CB * P)),
    }
    for l, (w, b) in enumerate([(g["L0_gnn_W1"].T, "L0_gnn_b1"), (g["L0_gnn_W2"].T, "L0_gnn_b2"),
                                (g["L1_gnn_weight"], "L1_gnn_bias"), (g["L3_gnn_W"].T, "L3_gnn_b")]):
        arrays[f"w{l}"] = w
        arrays[f"bias{l}"] = np.broadcast_to(g[b], (P, D))
    zero = np.zeros(D, np.float32)
    for r in range(2):
        wm, bm = g["L2_gnn_W_msg"][r], g["L2_gnn_b_msg"][r]
        arrays[f"wms{r}"] = wm[D:2 * D].T
        arrays[f"wmd{r}"] = np.concatenate([wm[0:D], wm[2 * D:], bm[None]]).T
        arrays[f"wih{r}"] = g["L2_gnn_W_ih"][r].T
        arrays[f"whh{r}"] = g["L2_gnn_W_hh"][r].T
        bi, bh = g["L2_gnn_b_ih"][r], g["L2_gnn_b_hh"][r]
        arrays[f"gbias{r}"] = np.stack([np.concatenate([bi, zero]), np.concatenate([bh[:2 * D], zero, bh[2 * D:]])])

    nc = bacc.Bacc("TRN2", target_bir_lowering=False, num_devices=1)
    feed, aps = {}, {}
    for name, a in arrays.items():
        feed[f"{name}_dram"] = np.ascontiguousarray(a)
        aps[name] = nc.dram_tensor(f"{name}_dram", a.shape, mybir.dt.from_np(a.dtype), kind="ExternalInput").ap()
    aps["out"] = nc.dram_tensor("out_dram", (N, D), mybir.dt.float32, kind="ExternalOutput").ap()
    build(nc, aps)
    r = run(nc, [feed], core_ids=[0])
    return r.results[0]["out_dram"]
```
